# Optimizing a Trainium2 kernel written in Bass

```python
import numpy as np
import jax
import jax.numpy as jnp

def _softmax(x, axis=-1):
    return jax.nn.softmax(x, axis=axis)

def _gelu(x):
    return jax.nn.gelu(x, approximate=True)

def _silu(x):
    return jax.nn.silu(x)

def _sigmoid(x):
    return jax.nn.sigmoid(x)

def _layernorm(x, axis=-1, eps=1e-05):
    m = jnp.mean(x, axis=axis, keepdims=True)
    v = jnp.var(x, axis=axis, keepdims=True)
    return (x - m) / jnp.sqrt(v + eps)

def _scatter_add(tgt, idx, src, axis=0):
    return tgt.at[idx].add(src)

def _segment_sum(src, seg, n):
    return jax.ops.segment_sum(src, seg, n)
kernel_name = 'mk_sandwich_d1_jaxref_r4_ea11cb'

def setup_inputs(seed: int=0):
    np.random.seed(seed)
    _w = jnp.asarray

    def _L0_attn_setup():
        import jax, jax.numpy as jnp
        import numpy as np
        D = 256
        K_LOW1 = D // 4
        K_LOW2 = D // 4

        def mix_precision_matmul(x, w):
            d = x.shape[-1]
            w1 = w[:K_LOW1]
            wh = w[K_LOW1:d - K_LOW2]
            w2 = w[d - K_LOW2:]
            y1 = jnp.matmul(x[..., :K_LOW1].astype(jnp.float16), w1.astype(jnp.float16)).astype(jnp.float32)
            yh = jnp.matmul(x[..., K_LOW1:d - K_LOW2], wh)
            y2 = jnp.matmul(x[..., d - K_LOW2:].astype(jnp.float16), w2.astype(jnp.float16)).astype(jnp.float32)
            return y1 + yh + y2
        key = jax.random.key(seed)
        k1, k2, k3, k4 = jax.random.split(key, 4)
        B, N, d = (8, 512, D)
        x = jax.random.normal(k1, (B, N, d), dtype=jnp.float32)
        weight_qkv = jax.random.normal(k2, (d, 3 * d), dtype=jnp.float32) * d ** (-0.5)
        out_w = jax.random.normal(k3, (d, d), dtype=jnp.float32) * d ** (-0.5)
        out_b = jax.random.normal(k4, (d,), dtype=jnp.float32) * 0.01
        return {'x': x, 'weight_qkv': weight_qkv, 'out_w': out_w, 'out_b': out_b}
    _L0_attn_in = _L0_attn_setup()

    def _L0_ffn_setup():
        import jax, jax.numpy as jnp
        import numpy as np
        DIM = 256

        def _reference_tuple_inner(x, W_r, W_k, W_v, mu_r, mu_k):
            B, T, C = x.shape
            x_prev = jnp.concatenate([jnp.zeros((B, 1, C), x.dtype), x[:, :-1, :]], axis=1)
            xr = mu_r * x + (1.0 - mu_r) * x_prev
            xk = mu_k * x + (1.0 - mu_k) * x_prev
            r = jax.nn.sigmoid(jnp.einsum('btc,dc->btd', xr, W_r))
            k = jnp.einsum('btc,dc->btd', xk, W_k)
            k_act = jnp.square(jax.nn.relu(k))
            out = r * jnp.einsum('btc,dc->btd', k_act, W_v)
            new_state = x[:, -1, :]
            return (out, new_state)
        key = jax.random.key(seed)
        ks = jax.random.split(key, 6)
        B, T, C = (8, 512, DIM)
        x = jax.random.normal(ks[0], (B, T, C), dtype=jnp.float32)
        s = 1.0 / np.sqrt(C)
        W_r = jax.random.uniform(ks[1], (C, C), jnp.float32, -s, s)
        W_k = jax.random.uniform(ks[2], (C, C), jnp.float32, -s, s)
        W_v = jax.random.uniform(ks[3], (C, C), jnp.float32, -s, s)
        mu_r = jax.random.uniform(ks[4], (C,), jnp.float32)
        mu_k = jax.random.uniform(ks[5], (C,), jnp.float32)
        return {'x': x, 'W_r': W_r, 'W_k': W_k, 'W_v': W_v, 'mu_r': mu_r, 'mu_k': mu_k}
    _L0_ffn_in = _L0_ffn_setup()
    _d = {'L0_attn_x': _L0_attn_in['x'], 'L0_attn_weight_qkv': _L0_attn_in['weight_qkv'], 'L0_attn_out_w': _L0_attn_in['out_w'], 'L0_attn_out_b': _L0_attn_in['out_b'], 'L0_ffn_W_r': _L0_ffn_in['W_r'], 'L0_ffn_W_k': _L0_ffn_in['W_k'], 'L0_ffn_W_v': _L0_ffn_in['W_v'], 'L0_ffn_mu_r': _L0_ffn_in['mu_r'], 'L0_ffn_mu_k': _L0_ffn_in['mu_k']}
    _x0 = _d['L0_attn_x']
    _d['L0_attn_x'] = jax.random.normal(jax.random.fold_in(jax.random.key(seed), 1), (4, 2048, 256), dtype=_x0.dtype)
    del _x0
    return _d

def reference(L0_attn_x, L0_attn_weight_qkv, L0_attn_out_w, L0_attn_out_b, L0_ffn_W_r, L0_ffn_W_k, L0_ffn_W_v, L0_ffn_mu_r, L0_ffn_mu_k):

    def _L0_attn_ref(x, weight_qkv, out_w, out_b):
        import jax, jax.numpy as jnp
        import numpy as np
        D = 256
        K_LOW1 = D // 4
        K_LOW2 = D // 4

        def mix_precision_matmul(x, w):
            d = x.shape[-1]
            w1 = w[:K_LOW1]
            wh = w[K_LOW1:d - K_LOW2]
            w2 = w[d - K_LOW2:]
            y1 = jnp.matmul(x[..., :K_LOW1].astype(jnp.float16), w1.astype(jnp.float16)).astype(jnp.float32)
            yh = jnp.matmul(x[..., K_LOW1:d - K_LOW2], wh)
            y2 = jnp.matmul(x[..., d - K_LOW2:].astype(jnp.float16), w2.astype(jnp.float16)).astype(jnp.float32)
            return y1 + yh + y2
        d = x.shape[-1]
        qkv = mix_precision_matmul(x, weight_qkv)
        q, k, v = jnp.split(qkv, 3, axis=-1)
        q = q / jnp.sqrt(jnp.asarray(d, dtype=q.dtype))
        qk = jnp.einsum('bqd,bkd->bqk', q, k)
        s = jax.nn.softmax(qk, axis=-1)
        y = jnp.einsum('bqk,bkd->bqd', s, v)
        return jnp.matmul(y, out_w.T) + out_b

    def _L0_ffn_ref(x, W_r, W_k, W_v, mu_r, mu_k):
        import jax, jax.numpy as jnp
        import numpy as np
        DIM = 256

        def _reference_tuple_inner(x, W_r, W_k, W_v, mu_r, mu_k):
            B, T, C = x.shape
            x_prev = jnp.concatenate([jnp.zeros((B, 1, C), x.dtype), x[:, :-1, :]], axis=1)
            xr = mu_r * x + (1.0 - mu_r) * x_prev
            xk = mu_k * x + (1.0 - mu_k) * x_prev
            r = jax.nn.sigmoid(jnp.einsum('btc,dc->btd', xr, W_r))
            k = jnp.einsum('btc,dc->btd', xk, W_k)
            k_act = jnp.square(jax.nn.relu(k))
            out = r * jnp.einsum('btc,dc->btd', k_act, W_v)
            new_state = x[:, -1, :]
            return (out, new_state)
        return _reference_tuple_inner(x, W_r, W_k, W_v, mu_r, mu_k)[0]
    x = L0_attn_x
    x = x + _layernorm(_L0_attn_ref(_layernorm(x, axis=-1), L0_attn_weight_qkv, L0_attn_out_w, L0_attn_out_b), axis=-1)
    x = x + _layernorm(_L0_ffn_ref(_layernorm(x, axis=-1), L0_ffn_W_r, L0_ffn_W_k, L0_ffn_W_v, L0_ffn_mu_r, L0_ffn_mu_k), axis=-1)
    return x

_drawn_inputs = setup_inputs


def setup_inputs(seed=0):
    import zlib

    import numpy as np

    out = dict(_drawn_inputs(seed))
    spreads = {}
    factors = {}
    for name, (base, spread) in spreads.items():
        noise = np.random.default_rng([zlib.crc32(name.encode()), seed]).standard_normal(out[name].shape)
        drawn = base * np.exp(spread * noise) if base else spread * noise
        out[name] = jnp.asarray(drawn.astype(out[name].dtype))
    for name, factor in factors.items():
        out[name] = (out[name] * factor).astype(out[name].dtype)
    return out
```

```python
from contextlib import ExitStack

import concourse.bass as bass
from concourse import mybir

F32 = mybir.dt.float32
F32R = mybir.dt.float32r
F16 = mybir.dt.float16
ALU = mybir.AluOpType
ACT = mybir.ActivationFunctionType

P = 128
BLK = 512
EPS = 1e-5


def sandwich(nc, x, w_qkv, out_w, out_b, w_r, w_k, w_v, mu_r, mu_k, out):
    NB, N, D = x.shape
    LOW = D // 4
    HALVES = D // P
    NJ = N // BLK
    NT = BLK // P
    NC = N // BLK
    NKT = N // P
    UNITS = NT * NC
    SCALE = float(D) ** -0.5
    RING = 3
    PRE = NJ
    assert D == 256 and N % BLK == 0

    xb = x.rearrange("b (j t p) d -> b j p t d", p=P, t=NT)
    ob = out.rearrange("b (j t p) d -> b j p t d", p=P, t=NT)

    ctx = ExitStack()
    with ctx:
        def sb(name, shape, dt=F32):
            return ctx.enter_context(nc.sbuf_tensor(name, shape, dt))

        def sem(name):
            return ctx.enter_context(nc.semaphore(name))

        def bank(name):
            return ctx.enter_context(nc.psum_tensor(name, [P, BLK], F32))

        ident = sb("ident", [P, P])
        wq_low = sb("wq_low", [P, 3 * D], F16)
        wq_hi = sb("wq_hi", [P, 3 * D], F32R)
        wq_lo = sb("wq_lo", [P, 3 * D], F32R)
        wt_hi = sb("wt_hi", [P, 4, HALVES, D], F32R)
        wt_lo = sb("wt_lo", [P, 4, HALVES, D], F32R)
        OUT, KEY, REC, VAL = range(4)
        bias_row = sb("bias_row", [P, D])
        mu = sb("mu", [P, 2, HALVES])
        one_minus_mu = sb("one_minus_mu", [P, 2, HALVES])
        minus_half = sb("minus_half", [P, NT])
        eps = sb("eps", [P, NT])

        xt_low = sb("xt_low", [P, N], F16)
        xt_hi = sb("xt_hi", [P, N], F32R)
        xt_lo = sb("xt_lo", [P, N], F32R)
        k_hi = sb("k_hi", [P, HALVES, N], F32R)
        k_lo = sb("k_lo", [P, HALVES, N], F32R)
        v_hi = sb("v_hi", [P, NKT, D], F32R)
        v_lo = sb("v_lo", [P, NKT, D], F32R)

        q_hi = sb("q_hi", [P, HALVES, BLK], F32R)
        q_lo = sb("q_lo", [P, HALVES, BLK], F32R)
        probs = sb("probs", [P, NT, N])
        WIDE = D + LOW
        xin = probs[:, :, :].rearrange("p a n -> p (a n)")[:, 0:NKT * WIDE].rearrange("p (t d) -> p t d", d=WIDE)
        chunk_max = sb("chunk_max", [P, NT, NC])
        scaled_max = sb("scaled_max", [P, NT, NC])
        neg_max = sb("neg_max", [P, NT])
        row_sum = sb("row_sum", [P, NT])
        inv_sum = sb("inv_sum", [P, NT])
        pt_hi = sb("pt_hi", [P, RING, BLK], F32R)
        pt_lo = sb("pt_lo", [P, RING, BLK], F32R)
        res = sb("res", [P, NT, D])
        att = sb("att", [P, NT, D])
        st = sb("st", [P, NT, 6])
        mv = sb("mv", [P, NT, 2])
        var_eps = sb("var_eps", [P, NT])
        rstd = sb("rstd", [P, NT])
        nmr = sb("nmr", [P, NT])
        pst = sb("pst", [P, NKT, 6])
        pmv = sb("pmv", [P, NKT, 2])
        pvar_eps = sb("pvar_eps", [P, NKT])
        prstd = sb("prstd", [P, NKT])
        xt = sb("xt", [P, HALVES, BLK + 1])
        tmp = sb("tmp", [P, HALVES, BLK])
        mixed = sb("mixed", [P, HALVES, BLK])
        xm_hi = sb("xm_hi", [P, 2, HALVES, BLK], F32R)
        xm_lo = sb("xm_lo", [P, 2, HALVES, BLK], F32R)
        yk_hi = sb("yk_hi", [P, HALVES, BLK], F32R)
        yk_lo = sb("yk_lo", [P, HALVES, BLK], F32R)

        S = [bank(f"S{i}") for i in range(2)]
        T = [bank(f"T{i}") for i in range(2)] + S
        Y = [bank(f"Y{i}") for i in range(HALVES)]
        M = [bank(f"M{i}") for i in range(2)]

        def f32(ap):
            return ap.bitcast(F32)

        w_in = sem("w_in"); mu_made = sem("mu_made"); vec_in = sem("vec_in"); x_in = [sem(f"x_in{i}") for i in range(PRE)]
        res_in = sem("res_in"); stored = sem("stored")
        ident_zero = sem("ident_zero"); ident_made = sem("ident_made"); consts_made = sem("consts_made")
        w_turned = sem("w_turned"); w_hi_made = sem("w_hi_made"); w_lo_made = sem("w_lo_made")
        pre_stats = sem("pre_stats"); pre_moments = sem("pre_moments"); pre_eps = sem("pre_eps")
        pre_rstd = sem("pre_rstd"); pre_normed = sem("pre_normed")
        x_turned = sem("x_turned"); xt_low_made = sem("xt_low_made"); xt_hi_made = sem("xt_hi_made")
        xt_lo_made = sem("xt_lo_made")
        kv_done = sem("kv_done"); kv_hi_made = sem("kv_hi_made"); kv_lo_made = sem("kv_lo_made")
        q_done = sem("q_done"); q_hi_made = sem("q_hi_made"); q_lo_made = sem("q_lo_made")
        s_done = sem("s_done"); s_copied = sem("s_copied"); max_made = sem("max_made"); exp_made = sem("exp_made")
        p_turned = sem("p_turned"); pt_hi_made = sem("pt_hi_made"); pt_lo_made = sem("pt_lo_made")
        pv_done = sem("pv_done"); y_hi_made = sem("y_hi_made"); y_lo_made = sem("y_lo_made")
        inv_made = sem("inv_made"); o_done = sem("o_done"); att_made = sem("att_made")
        stats = sem("stats"); moments = sem("moments"); eps_added = sem("eps_added"); rstd_made = sem("rstd_made")
        att_normed = sem("att_normed"); res_made = sem("res_made"); mix_in_made = sem("mix_in_made")
        mix_in_turned = sem("mix_in_turned"); xt_made = sem("xt_made"); carried = sem("carried")
        prev_part = sem("prev_part"); mixed_made = sem("mixed_made"); xm_hi_made = sem("xm_hi_made")
        xm_lo_made = sem("xm_lo_made")
        key_done = sem("key_done"); relu_made = sem("relu_made"); sq_made = sem("sq_made")
        sq_hi_made = sem("sq_hi_made"); sq_lo_made = sem("sq_lo_made")
        rec_done = sem("rec_done"); rec_exp = sem("rec_exp"); rec_plus = sem("rec_plus"); rec_made = sem("rec_made")
        val_done = sem("val_done"); f_made = sem("f_made"); nmr_made = sem("nmr_made"); f_normed = sem("f_normed")
        out_made = sem("out_made")
        waited = sem("waited")

        stage_low = probs[:, 0, 0:3 * D]
        stage_mid = probs[:, 0, 3 * D:6 * D]
        stage_w = probs[:, 1, :].rearrange("p (w h c) -> p w h c", w=4, h=HALVES)

        def kv_place(hi, j, n):
            if n < HALVES:
                return (k_hi if hi else k_lo)[:, n, j * BLK:(j + 1) * BLK]
            t = j * NT + 2 * (n - HALVES)
            return (v_hi if hi else v_lo)[:, t:t + 2, :]

        KV = M + S

        block = ctx.enter_context(nc.Block())

        @block.sync
        def _(sp):
            sp.dma_start(stage_low[0:LOW, :], w_qkv[D - LOW:D, :]).then_inc(w_in, 16)
            sp.dma_start(stage_low[LOW:P, :], w_qkv[0:LOW, :]).then_inc(w_in, 16)
            sp.dma_start(stage_mid, w_qkv[LOW:D - LOW, :]).then_inc(w_in, 16)
            for i, w in ((OUT, out_w), (KEY, w_k), (REC, w_r), (VAL, w_v)):
                sp.dma_start(stage_w[:, i], w.rearrange("(h p) c -> p h c", p=P)).then_inc(w_in, 16)
            sp.dma_start(bias_row[:, :], out_b.rearrange("(a n) -> a n", a=1).broadcast_to([P, D])).then_inc(vec_in, 16)
            for i, m in enumerate((mu_k, mu_r)):
                for h in range(HALVES):
                    sp.dma_start(mu[:, i, h:h + 1], m[h * P:(h + 1) * P].rearrange("(p a) -> p a", a=1)).then_inc(vec_in, 16)
            with sp.Fori(0, NB) as b:
                sp.wait_ge(w_turned, 4)
                sp.wait_ge(w_hi_made, 6)
                sp.wait_ge(w_lo_made, 5)
                for j in range(PRE):
                    sp.dma_start(xin[:, j * NT:(j + 1) * NT, 0:D], xb[b, j]).then_inc(x_in[j], 16)
                    sp.dma_start(xin[:, j * NT:(j + 1) * NT, D:WIDE], xb[b, j, :, :, 0:LOW]).then_inc(x_in[j], 16)
                with sp.Fori(0, NJ) as j:
                    sp.dma_start(res[:, :, :], xb[b, j]).then_inc(res_in, 16)
                    sp.wait_ge(out_made, (b * NJ + j) * NT + NT)
                    sp.dma_start(ob[b, j], att[:, :, :]).then_inc(stored, 16)
                    sp.wait_ge(stored, (b * NJ + j + 1) * 16)
                    sp.sem_inc(waited, 1)

        @block.gpsimd
        def _(pool):
            pool.memset(ident[:, :], 0.0).then_inc(ident_zero, 1)
            pool.memset(minus_half[:, :], -0.5).then_inc(consts_made, 1)
            pool.memset(eps[:, :], EPS).then_inc(consts_made, 1)
            pool.wait_ge(ident_zero, 1)
            pool.affine_select(out=ident[:, :], in_=ident[:, :], compare_op=ALU.not_equal, fill=1.0, base=0,
                               pattern=[[-1, P]], channel_multiplier=1).then_inc(ident_made, 1)
            pool.wait_ge(consts_made, 2)

            def rsqrt(g3):
                pool.wait_ge(moments, (g3 + 1) * NT)
                pool.tensor_tensor(var_eps[:, :], mv[:, :, 1], eps[:, :], ALU.add).then_inc(eps_added, 1)
                pool.wait_ge(eps_added, g3 + 1)
                pool.tensor_tensor(rstd[:, :], var_eps[:, :], minus_half[:, :], ALU.pow).then_inc(rstd_made, 1)

            def post(g, carries):
                pool.wait_ge(res_in, (g + 1) * 16)
                rsqrt(g * 3)
                for t in range(NT):
                    pool.wait_ge(att_normed, g * NT + t + 1)
                    pool.tensor_tensor(res[:, t, :], res[:, t, :], att[:, t, :], ALU.add).then_inc(res_made, 1)
                rsqrt(g * 3 + 1)
                for n in range(2 * HALVES):
                    i, h = divmod(n, HALVES)
                    pool.wait_ge(mixed_made, g * 4 + n + 1)
                    pool.sem_inc(waited, 1)
                    pool.tensor_copy(xm_hi[:, i, h, :], mixed[:, h, :]).then_inc(xm_hi_made, 1)
                    pool.wait_ge(xm_hi_made, g * 4 + n + 1)
                    pool.tensor_tensor(xm_lo[:, i, h, :], mixed[:, h, :], f32(xm_hi[:, i, h, :]),
                                       ALU.subtract).then_inc(xm_lo_made, 1)
                pool.tensor_copy(xt[:, :, 0:1], xt[:, :, BLK:BLK + 1]).then_inc(carried, 1)
                for m in range(HALVES):
                    pool.wait_ge(sq_made, g * 2 + m + 1)
                    pool.sem_inc(waited, 1)
                    pool.tensor_copy(yk_hi[:, m, :], mixed[:, m, :]).then_inc(sq_hi_made, 1)
                    pool.wait_ge(sq_hi_made, g * 2 + m + 1)
                    pool.tensor_tensor(yk_lo[:, m, :], mixed[:, m, :], f32(yk_hi[:, m, :]),
                                       ALU.subtract).then_inc(sq_lo_made, 1)
                rsqrt(g * 3 + 2)
                pool.wait_ge(rstd_made, g * 3 + 3)
                pool.tensor_tensor(nmr[:, :], mv[:, :, 0], rstd[:, :], ALU.mult).then_inc(nmr_made, 1)
                pool.wait_ge(nmr_made, g + 1)
                pool.sem_inc(waited, 1)
                for t in range(NT):
                    pool.tensor_scalar(att[:, t, :], att[:, t, :], rstd[:, t:t + 1], nmr[:, t:t + 1],
                                       ALU.mult, ALU.subtract).then_inc(f_normed, 1)
                for t in range(NT):
                    pool.wait_ge(f_normed, g * NT + t + 1)
                    pool.tensor_tensor(att[:, t, :], att[:, t, :], res[:, t, :], ALU.add).then_inc(out_made, 1)

            with pool.Fori(0, NB) as b:
                for j in range(PRE):
                    r = slice(j * NT, (j + 1) * NT)
                    pool.wait_ge(pre_moments, b * NKT + (j + 1) * NT)
                    pool.tensor_tensor(pvar_eps[:, r], pmv[:, r, 1], eps[:, :], ALU.add).then_inc(pre_eps, 1)
                    pool.wait_ge(pre_eps, b * PRE + j + 1)
                    pool.tensor_tensor(prstd[:, r], pvar_eps[:, r], minus_half[:, :], ALU.pow).then_inc(pre_rstd, 1)
                pool.memset(xt[:, :, 0:1], 0.0).then_inc(carried, 1)
                with pool.Fori(0, NJ) as j:
                    post(b * NJ + j, j)

        @block.scalar
        def _(act):
            def copy(out_, in_):
                return act.activation(out_, in_, ACT.Copy)

            act.wait_ge(mu_made, 1)
            act.wait_ge(w_in, 7 * 16)
            copy(wq_low[:, :], stage_low).then_inc(w_hi_made, 1)
            copy(wq_hi[:, :], stage_mid).then_inc(w_hi_made, 1)
            for i in range(4):
                act.wait_ge(w_turned, i + 1)
                copy(wt_hi[:, i], (S + M)[i][:, :]).then_inc(w_hi_made, 1)

            def q_split(g):
                for m in range(HALVES):
                    act.wait_ge(q_done, g * 2 + m + 1)
                    copy(q_hi[:, m, :], S[m][:, :]).then_inc(q_hi_made, 1)

            def softmax_exp(g, t):
                act.wait_ge(max_made, g * NT + t + 1)
                act.activation(probs[:, t, :], probs[:, t, :], ACT.Exp, bias=neg_max[:, t:t + 1], scale=SCALE,
                               accum_out=row_sum[:, t:t + 1]).then_inc(exp_made, 1)

            def mix_values(g):
                for kt in range(NKT):
                    act.wait_ge(p_turned, g * NKT + kt + 1)
                    if kt >= RING:
                        act.wait_ge(pv_done, g * NKT + kt - RING + 1)
                    copy(pt_hi[:, kt % RING, :], T[kt % 4][:, :]).then_inc(pt_hi_made, 1)

            def post(g, exps):
                act.wait_ge(pv_done, (g + 1) * NKT)
                for m in range(HALVES):
                    copy(yk_hi[:, m, :], Y[m][:, :]).then_inc(y_hi_made, 1)
                if exps:
                    softmax_exp(g + 1, 0)
                    softmax_exp(g + 1, 1)
                    softmax_exp(g + 1, 2)
                act.wait_ge(carried, g_carried(g))
                for h in range(HALVES):
                    act.wait_ge(mix_in_turned, g * 2 + h + 1)
                    copy(xt[:, h, 1:BLK + 1], M[h][:, :]).then_inc(xt_made, 1)
                for n in range(2 * HALVES):
                    i, h = divmod(n, HALVES)
                    act.wait_ge(xt_made, g * 2 + h + 1)
                    if i == 1:
                        act.wait_ge(mixed_made, g * 4 + h + 1)
                    act.activation(tmp[:, h, :], xt[:, h, 0:BLK], ACT.Copy,
                                   scale=one_minus_mu[:, i, h:h + 1]).then_inc(prev_part, 1)
                act.wait_ge(mixed_made, g * 4 + 4)
                if exps:
                    softmax_exp(g + 1, 3)
                for m in range(HALVES):
                    act.wait_ge(key_done, g * 2 + m + 1)
                    act.activation(tmp[:, m, :], M[m][:, :], ACT.Relu).then_inc(relu_made, 1)
                for i in range(2):
                    act.wait_ge(rec_done, g * 2 + i + 1)
                    act.activation(tmp[:, i, :], M[i][:, :], ACT.Exp, scale=-1.0).then_inc(rec_exp, 1)

            def kv_split(b, j):
                for n in range(4):
                    act.wait_ge(kv_done, b * (4 * PRE) + 4 * j + n + 1)
                    src = KV[n][:, :] if n < HALVES else KV[n][:, :].rearrange("p (t d) -> p t d", t=2)
                    copy(kv_place(True, j, n), src).then_inc(kv_hi_made, 1)

            state = {}

            def g_carried(g):
                return g + state["b"] + 1

            with act.Fori(0, NB) as b:
                state["b"] = b
                for j in range(PRE):
                    act.wait_ge(x_turned, b * PRE + j + 1)
                    cols = slice(j * BLK, (j + 1) * BLK)
                    copy(xt_low[:, cols], T[0][:, :]).then_inc(xt_low_made, 1)
                    copy(xt_hi[:, cols], T[1][:, :]).then_inc(xt_hi_made, 1)
                    if j:
                        kv_split(b, j - 1)
                kv_split(b, PRE - 1)
                q_split(b * NJ)
                for t in range(NT):
                    softmax_exp(b * NJ, t)
                with act.Fori(0, NJ - 1) as j:
                    q_split(b * NJ + j + 1)
                    mix_values(b * NJ + j)
                    post(b * NJ + j, True)
                mix_values(b * NJ + NJ - 1)
                post(b * NJ + NJ - 1, False)

        @block.vector
        def _(dve):
            def low_part(out_lo, psum, hi):
                return dve.tensor_tensor(out_lo, psum, f32(hi), ALU.subtract)

            dve.wait_ge(vec_in, (1 + 2 * HALVES) * 16)
            dve.tensor_scalar(one_minus_mu[:, :, :], mu[:, :, :], -1.0, 1.0, ALU.mult, ALU.add).then_inc(mu_made, 1)
            dve.wait_ge(w_hi_made, 2)
            low_part(wq_lo[:, :], stage_mid, wq_hi[:, :]).then_inc(w_lo_made, 1)
            for i in range(4):
                dve.wait_ge(w_hi_made, 3 + i)
                low_part(wt_lo[:, i], (S + M)[i][:, :].rearrange("p (h d) -> p h d", h=HALVES),
                         wt_hi[:, i]).then_inc(w_lo_made, 1)

            def pre_stat(b, j):
                dve.wait_ge(x_in[j], (b + 1) * 32)
                for t in range(j * NT, (j + 1) * NT):
                    dve.bn_stats(pst[:, t, :], xin[:, t, 0:D]).then_inc(pre_stats, 1)
                dve.wait_ge(pre_stats, b * NKT + (j + 1) * NT)
                dve.sem_inc(waited, 1)
                for t in range(j * NT, (j + 1) * NT):
                    dve.bn_aggr(pmv[:, t, :], pst[:, t, :]).then_inc(pre_moments, 1)

            def pre_norm(b, j):
                dve.wait_ge(pre_rstd, b * PRE + j + 1)
                for t in range(j * NT, (j + 1) * NT):
                    dve.tensor_scalar(xin[:, t, :], xin[:, t, :], pmv[:, t, 0:1], prstd[:, t:t + 1],
                                      ALU.subtract, ALU.mult).then_inc(pre_normed, 1)

            def x_low(b, j):
                cols = slice(j * BLK, (j + 1) * BLK)
                dve.wait_ge(xt_hi_made, b * PRE + j + 1)
                low_part(xt_lo[:, cols], T[1][:, :], xt_hi[:, cols]).then_inc(xt_lo_made, 1)

            def kv_low(b, j):
                for n in range(4):
                    dve.wait_ge(kv_hi_made, b * (4 * PRE) + 4 * j + n + 1)
                    src = KV[n][:, :] if n < HALVES else KV[n][:, :].rearrange("p (t d) -> p t d", t=2)
                    low_part(kv_place(False, j, n), src, kv_place(True, j, n)).then_inc(kv_lo_made, 1)

            def q_low(g):
                for m in range(HALVES):
                    dve.wait_ge(q_hi_made, g * 2 + m + 1)
                    low_part(q_lo[:, m, :], S[m][:, :], q_hi[:, m, :]).then_inc(q_lo_made, 1)

            def scores_out(g, u):
                t, c = divmod(u, NC)
                dve.wait_ge(s_done, g * UNITS + u + 1)
                dve.tensor_scalar(probs[:, t, c * BLK:(c + 1) * BLK], S[u % 2][:, :], 1.0, None, ALU.mult, ALU.max,
                                  accum_out=chunk_max[:, t, c:c + 1]).then_inc(s_copied, 1)
                if c == NC - 1:
                    dve.wait_ge(s_copied, g * UNITS + u + 1)
                    dve.tensor_scalar(scaled_max[:, t, :], chunk_max[:, t, :], -SCALE, None, ALU.mult, ALU.min,
                                      accum_out=neg_max[:, t:t + 1]).then_inc(max_made, 1)

            def mix_values(g):
                for kt in range(NKT):
                    dve.wait_ge(pt_hi_made, g * NKT + kt + 1)
                    low_part(pt_lo[:, kt % RING, :], T[kt % 4][:, :], pt_hi[:, kt % RING, :]).then_inc(pt_lo_made, 1)

            def tile_stats(src, n3, ts):
                for t in ts:
                    dve.bn_stats(st[:, t, :], src[:, t, :]).then_inc(stats, 1)

            def tile_moments(n3):
                dve.wait_ge(stats, (n3 + 1) * NT)
                dve.sem_inc(waited, 1)
                for t in range(NT):
                    dve.bn_aggr(mv[:, t, :], st[:, t, :]).then_inc(moments, 1)

            def post(g, scores):
                def y_low(m):
                    dve.wait_ge(y_hi_made, g * 2 + m + 1)
                    low_part(yk_lo[:, m, :], Y[m][:, :], yk_hi[:, m, :]).then_inc(y_lo_made, 1)

                def attention(t):
                    dve.wait_ge(o_done, g * 2 + t // 2 + 1)
                    dve.wait_ge(res_in, (g + 1) * 16)
                    dve.wait_ge(inv_made, g + 1)
                    dve.scalar_tensor_tensor(out=att[:, t, :], in0=M[t // 2][:, (t % 2) * D:(t % 2 + 1) * D],
                                             scalar=inv_sum[:, t:t + 1], in1=bias_row[:, :],
                                             op0=ALU.mult, op1=ALU.add).then_inc(att_made, 1)

                def mixes(n):
                    i, h = divmod(n, HALVES)
                    dve.wait_ge(prev_part, g * 4 + n + 1)
                    if i == 1:
                        dve.wait_ge(xm_lo_made, g * 4 + h + 1)
                    dve.scalar_tensor_tensor(out=mixed[:, h, :], in0=xt[:, h, 1:BLK + 1], scalar=mu[:, i, h:h + 1],
                                             in1=tmp[:, h, :], op0=ALU.mult, op1=ALU.add).then_inc(mixed_made, 1)

                scores(0)
                y_low(0)
                scores(1)
                y_low(1)
                dve.reciprocal(inv_sum[:, :], row_sum[:, :]).then_inc(inv_made, 1)
                scores(2)
                scores(3)
                for t in range(NT):
                    attention(t)
                    if t:
                        dve.wait_ge(att_made, g * NT + t)
                        tile_stats(att, g * 3, [t - 1])
                    if t < 2:
                        scores(4 + t)
                dve.wait_ge(att_made, g * NT + NT)
                tile_stats(att, g * 3, [NT - 1])
                scores(6)
                tile_moments(g * 3)
                scores(7)
                dve.wait_ge(rstd_made, g * 3 + 1)
                for t in range(NT):
                    dve.tensor_scalar(att[:, t, :], att[:, t, :], mv[:, t, 0:1], rstd[:, t:t + 1],
                                      ALU.subtract, ALU.mult).then_inc(att_normed, 1)
                scores(8)
                scores(9)
                for t in range(NT):
                    dve.wait_ge(res_made, g * NT + t + 1)
                    tile_stats(res, g * 3 + 1, [t])
                tile_moments(g * 3 + 1)
                scores(10)
                scores(11)
                dve.wait_ge(rstd_made, g * 3 + 2)
                for t in range(NT):
                    dve.tensor_scalar(att[:, t, :], res[:, t, :], mv[:, t, 0:1], rstd[:, t:t + 1],
                                      ALU.subtract, ALU.mult).then_inc(mix_in_made, 1)
                scores(12)
                scores(13)
                mixes(0)
                scores(14)
                mixes(1)
                scores(15)
                mixes(2)
                mixes(3)
                for m in range(HALVES):
                    dve.wait_ge(relu_made, g * 2 + m + 1)
                    dve.wait_ge(xm_lo_made, g * 4 + 4)
                    dve.tensor_tensor(mixed[:, m, :], M[m][:, :], tmp[:, m, :], ALU.mult).then_inc(sq_made, 1)
                for i in range(2):
                    dve.wait_ge(rec_exp, g * 2 + i + 1)
                    dve.tensor_scalar(tmp[:, i, :], tmp[:, i, :], 1.0, None, ALU.add).then_inc(rec_plus, 1)
                for i in range(2):
                    dve.wait_ge(rec_plus, g * 2 + i + 1)
                    dve.reciprocal(tmp[:, i, :], tmp[:, i, :]).then_inc(rec_made, 1)
                for i in range(2):
                    dve.wait_ge(val_done, g * 2 + i + 1)
                    dve.wait_ge(rec_made, g * 2 + i + 1)
                    dve.tensor_tensor(att[:, 2 * i:2 * i + 2, :], M[i][:, :].rearrange("p (t d) -> p t d", t=2),
                                      tmp[:, i, :].rearrange("p (t d) -> p t d", t=2), ALU.mult).then_inc(f_made, 1)
                for t in range(NT):
                    dve.wait_ge(f_made, g * 2 + t // 2 + 1)
                    tile_stats(att, g * 3 + 2, [t])
                tile_moments(g * 3 + 2)

            with dve.Fori(0, NB) as b:
                pre_stat(b, 0)
                pre_stat(b, 1)
                pre_norm(b, 0)
                pre_stat(b, 2)
                pre_norm(b, 1)
                x_low(b, 0)
                pre_stat(b, 3)
                pre_norm(b, 2)
                x_low(b, 1)
                kv_low(b, 0)
                pre_norm(b, 3)
                x_low(b, 2)
                kv_low(b, 1)
                x_low(b, 3)
                kv_low(b, 2)
                kv_low(b, 3)
                q_low(b * NJ)
                for u in range(UNITS):
                    scores_out(b * NJ, u)
                with dve.Fori(0, NJ - 1) as j:
                    g = b * NJ + j
                    q_low(g + 1)
                    mix_values(g)
                    post(g, lambda u: scores_out(g + 1, u))
                mix_values(b * NJ + NJ - 1)
                post(b * NJ + NJ - 1, lambda u: None)

        @block.tensor
        def _(pe):
            def three(out_, a_hi, a_lo, b_hi, b_lo, start, stop):
                pe.matmul(out_, a_hi, b_hi, start=start, stop=False)
                pe.matmul(out_, a_hi, b_lo, start=False, stop=False)
                return pe.matmul(out_, a_lo, b_hi, start=False, stop=stop)

            pe.wait_ge(w_in, 7 * 16)
            pe.wait_ge(ident_made, 1)
            for i in range(4):
                for h in range(HALVES):
                    for e in range(HALVES):
                        mm = pe.transpose((S + M)[i][:, h * D + e * P:h * D + (e + 1) * P],
                                          stage_w[:, i, e, h * P:(h + 1) * P], ident[:, :])
                mm.then_inc(w_turned, 1)
            pe.wait_ge(w_lo_made, 5)

            def turn_x(b, j):
                pe.wait_ge(pre_normed, b * NKT + (j + 1) * NT)
                if j:
                    pe.wait_ge(xt_lo_made, b * PRE + j)
                for t in range(NT):
                    row = xin[:, j * NT + t, :]
                    pe.transpose(T[0][:, t * P:(t + 1) * P], row[:, D - LOW:WIDE], ident[:, :])
                    mm = pe.transpose(T[1][:, t * P:(t + 1) * P], row[:, LOW:D - LOW], ident[:, :])
                mm.then_inc(x_turned, 1)

            def project(out_, w_cols, x_cols):
                pe.matmul(out_, wq_low[:, w_cols], xt_low[:, x_cols], start=True, stop=False)
                return three(out_, wq_hi[:, w_cols], wq_lo[:, w_cols], xt_hi[:, x_cols], xt_lo[:, x_cols], False, True)

            def keys_values(b, j):
                pe.wait_ge(xt_low_made, b * PRE + j + 1)
                pe.wait_ge(xt_lo_made, b * PRE + j + 1)
                for n in range(4):
                    if j:
                        pe.wait_ge(kv_lo_made, b * (4 * PRE) + 4 * (j - 1) + n + 1)
                    if n < HALVES:
                        mm = project(KV[n][:, :], slice(D + n * P, D + (n + 1) * P), slice(j * BLK, (j + 1) * BLK))
                    else:
                        for i in range(2):
                            t = j * NT + 2 * (n - HALVES) + i
                            rows, cols = slice(t * P, (t + 1) * P), slice(2 * D, 3 * D)
                            o = KV[n][:, i * D:(i + 1) * D]
                            pe.matmul(o, xt_low[:, rows], wq_low[:, cols], start=True, stop=False)
                            mm = three(o, xt_hi[:, rows], xt_lo[:, rows], wq_hi[:, cols], wq_lo[:, cols], False, True)
                    mm.then_inc(kv_done, 1)

            def queries(g, j):
                for m in range(HALVES):
                    project(S[m][:, :], slice(m * P, (m + 1) * P), bass.ds(j * BLK, BLK)).then_inc(q_done, 1)

            def scores(g, u):
                t, c = divmod(u, NC)
                if u >= 2:
                    pe.wait_ge(s_copied, g * UNITS + u - 1)
                rows, cols = slice(t * P, (t + 1) * P), slice(c * BLK, (c + 1) * BLK)
                for m in range(HALVES):
                    mm = three(S[u % 2][:, :], q_hi[:, m, rows], q_lo[:, m, rows], k_hi[:, m, cols], k_lo[:, m, cols],
                               m == 0, m == HALVES - 1)
                mm.then_inc(s_done, 1)

            def turn_probs(g, kt):
                for t in range(NT):
                    mm = pe.transpose(T[kt % 4][:, t * P:(t + 1) * P], probs[:, t, kt * P:(kt + 1) * P], ident[:, :])
                mm.then_inc(p_turned, 1)

            def mix_values(g):
                pe.wait_ge(exp_made, (g + 1) * NT)
                for kt in range(3):
                    turn_probs(g, kt)
                for kt in range(NKT):
                    pe.wait_ge(pt_lo_made, g * NKT + kt + 1)
                    s = kt % RING
                    for m in range(HALVES):
                        cols = slice(m * P, (m + 1) * P)
                        mm = three(Y[m][:, :], v_hi[:, kt, cols], v_lo[:, kt, cols], pt_hi[:, s, :], pt_lo[:, s, :],
                                   kt == 0, kt == NKT - 1)
                    mm.then_inc(pv_done, 1)
                    if kt + 3 < NKT:
                        turn_probs(g, kt + 3)

            def by_rows(a_hi, a_lo, w, done):
                for t in range(NT):
                    rows = slice(t * P, (t + 1) * P)
                    for h in range(HALVES):
                        mm = three(M[t // 2][:, (t % 2) * D:(t % 2 + 1) * D], a_hi[:, h, rows], a_lo[:, h, rows],
                                   wt_hi[:, w, h, :], wt_lo[:, w, h, :], h == 0, h == HALVES - 1)
                    if t % 2:
                        mm.then_inc(done, 1)

            def post(g, scores):
                for u in range(3):
                    scores(u)
                pe.wait_ge(y_lo_made, g * 2 + 2)
                by_rows(yk_hi, yk_lo, OUT, o_done)
                for u in range(3, 13):
                    scores(u)
                pe.wait_ge(mix_in_made, g * NT + NT)
                for h in range(HALVES):
                    for t in range(NT):
                        mm = pe.transpose(M[h][:, t * P:(t + 1) * P], att[:, t, h * P:(h + 1) * P], ident[:, :])
                    mm.then_inc(mix_in_turned, 1)
                for u in range(13, 16):
                    scores(u)
                pe.wait_ge(xm_lo_made, g * 4 + 2)
                for m in range(HALVES):
                    cols = slice(m * P, (m + 1) * P)
                    for h in range(HALVES):
                        mm = three(M[m][:, :], wt_hi[:, KEY, h, cols], wt_lo[:, KEY, h, cols], xm_hi[:, 0, h, :],
                                   xm_lo[:, 0, h, :], h == 0, h == HALVES - 1)
                    mm.then_inc(key_done, 1)
                pe.wait_ge(xm_lo_made, g * 4 + 4)
                pe.wait_ge(sq_made, g * 2 + 2)
                by_rows(xm_hi[:, 1], xm_lo[:, 1], REC, rec_done)
                pe.wait_ge(sq_lo_made, g * 2 + 2)
                pe.wait_ge(rec_exp, g * 2 + 2)
                by_rows(yk_hi, yk_lo, VAL, val_done)

            with pe.Fori(0, NB) as b:
                turn_x(b, 0)
                for j in range(PRE):
                    if j + 1 < PRE:
                        turn_x(b, j + 1)
                    keys_values(b, j)
                pe.wait_ge(kv_lo_made, (b + 1) * (4 * PRE))
                queries(b * NJ, 0)
                pe.wait_ge(q_lo_made, (b * NJ + 1) * 2)
                for u in range(UNITS):
                    scores(b * NJ, u)
                with pe.Fori(0, NJ - 1) as j:
                    g = b * NJ + j
                    pe.wait_ge(s_copied, (g + 1) * UNITS)
                    queries(g + 1, j + 1)
                    pe.wait_ge(q_lo_made, (g + 2) * 2)
                    mix_values(g)
                    post(g, lambda u: scores(g + 1, u))
                mix_values(b * NJ + NJ - 1)
                post(b * NJ + NJ - 1, lambda u: None)


_INS = ["L0_attn_x", "L0_attn_weight_qkv", "L0_attn_out_w", "L0_attn_out_b", "L0_ffn_W_r", "L0_ffn_W_k",
        "L0_ffn_W_v", "L0_ffn_mu_r", "L0_ffn_mu_k"]


def kernel(**inputs):
    import numpy as np
    import concourse.bacc as bacc
    from concourse.bass_utils import run_bass_kernel_spmd

    nc = bacc.Bacc("TRN2", target_bir_lowering=False, num_devices=1)
    arrays, args = {}, []
    for name in _INS:
        a = np.ascontiguousarray(inputs[name])
        arrays[f"in_{name}"] = a
        args.append(nc.dram_tensor(f"in_{name}", a.shape, mybir.dt.from_np(a.dtype), kind="ExternalInput").ap())
    shape = arrays["in_L0_attn_x"].shape
    out = nc.dram_tensor("out_x", shape, F32, kind="ExternalOutput").ap()
    sandwich(nc, *args, out)
    r = run_bass_kernel_spmd(nc, [arrays], core_ids=[0])
    return r.results[0]["out_x"]
```

```python
from contextlib import ExitStack

import concourse.bass as bass
from concourse import mybir

F32 = mybir.dt.float32
F32R = mybir.dt.float32r
F16 = mybir.dt.float16
ALU = mybir.AluOpType
ACT = mybir.ActivationFunctionType

P = 128
BLK = 512
EPS = 1e-5


def sandwich(nc, x, w_qkv, out_w, out_b, w_r, w_k, w_v, mu_r, mu_k, out):
    NB, N, D = x.shape
    LOW = D // 4
    HALVES = D // P
    NJ = N // BLK
    NT = BLK // P
    NC = N // BLK
    NKT = N // P
    UNITS = NT * NC
    SCALE = float(D) ** -0.5
    RING = 3
    PRE = NJ
    assert D == 256 and N % BLK == 0

    xb = x.rearrange("b (j t p) d -> b j p t d", p=P, t=NT)
    ob = out.rearrange("b (j t p) d -> b j p t d", p=P, t=NT)

    ctx = ExitStack()
    with ctx:
        def sb(name, shape, dt=F32):
            return ctx.enter_context(nc.sbuf_tensor(name, shape, dt))

        def sem(name):
            return ctx.enter_context(nc.semaphore(name))

        def bank(name):
            return ctx.enter_context(nc.psum_tensor(name, [P, BLK], F32))

        ident = sb("ident", [P, P])
        wq_low = sb("wq_low", [P, 3 * D], F16)
        wq_hi = sb("wq_hi", [P, 3 * D], F32R)
        wq_lo = sb("wq_lo", [P, 3 * D], F32R)
        wt_hi = sb("wt_hi", [P, 4, HALVES, D], F32R)
        wt_lo = sb("wt_lo", [P, 4, HALVES, D], F32R)
        OUT, KEY, REC, VAL = range(4)
        bias_row = sb("bias_row", [P, D])
        mu = sb("mu", [P, 2, HALVES])
        one_minus_mu = sb("one_minus_mu", [P, 2, HALVES])
        minus_half = sb("minus_half", [P, NT])
        eps = sb("eps", [P, NT])

        xin = sb("xin", [P, 2, NT, D])
        xt_low = sb("xt_low", [P, N], F16)
        xt_hi = sb("xt_hi", [P, N], F32R)
        xt_lo = sb("xt_lo", [P, N], F32R)
        k_hi = sb("k_hi", [P, HALVES, N], F32R)
        k_lo = sb("k_lo", [P, HALVES, N], F32R)
        v_hi = sb("v_hi", [P, NKT, D], F32R)
        v_lo = sb("v_lo", [P, NKT, D], F32R)

        q_hi = sb("q_hi", [P, HALVES, BLK], F32R)
        q_lo = sb("q_lo", [P, HALVES, BLK], F32R)
        probs = sb("probs", [P, NT, N])
        chunk_max = sb("chunk_max", [P, NT, NC])
        scaled_max = sb("scaled_max", [P, NT, NC])
        neg_max = sb("neg_max", [P, NT])
        part_sum = sb("part_sum", [P, 2])
        sum_copy = sb("sum_copy", [P, 2])
        row_sum = sb("row_sum", [P, NT])
        inv_sum = sb("inv_sum", [P, NT])
        pt_hi = sb("pt_hi", [P, RING, BLK], F32R)
        pt_lo = sb("pt_lo", [P, RING, BLK], F32R)
        res = sb("res", [P, NT, D])
        att = sb("att", [P, NT, D])
        st = sb("st", [P, NT, 6])
        mv = sb("mv", [P, NT, 2])
        var_eps = sb("var_eps", [P, NT])
        rstd = sb("rstd", [P, NT])
        pst = sb("pst", [P, NT, 6])
        pmv = sb("pmv", [P, NT, 2])
        pvar_eps = sb("pvar_eps", [P, NT])
        prstd = sb("prstd", [P, NT])
        xt = sb("xt", [P, HALVES, BLK + 1])
        tmp = sb("tmp", [P, HALVES, BLK])
        mixed = sb("mixed", [P, HALVES, BLK])
        xm_hi = sb("xm_hi", [P, HALVES, BLK], F32R)
        xm_lo = sb("xm_lo", [P, HALVES, BLK], F32R)
        yk_hi = sb("yk_hi", [P, HALVES, BLK], F32R)
        yk_lo = sb("yk_lo", [P, HALVES, BLK], F32R)

        S = [bank(f"S{i}") for i in range(2)]
        T01 = [bank(f"T{i}") for i in range(2)]
        T = T01 + S
        Y = [bank(f"Y{i}") for i in range(HALVES)]
        M = [bank(f"M{i}") for i in range(2)]

        def f32(ap):
            return ap.bitcast(F32)

        def pair(ap):
            return ap.rearrange("p (t d) -> p t d", t=2)

        w_in = sem("w_in"); mu_made = sem("mu_made"); vec_in = sem("vec_in")
        x_in = [sem(f"x_in{i}") for i in range(2)]
        res_in = sem("res_in"); stored = sem("stored"); att_free = sem("att_free")
        ident_zero = sem("ident_zero"); ident_made = sem("ident_made"); consts_made = sem("consts_made")
        w_turned = sem("w_turned"); w_hi_made = sem("w_hi_made"); w_lo_made = sem("w_lo_made")
        pre_stats = sem("pre_stats"); pre_moments = sem("pre_moments"); pre_eps = sem("pre_eps")
        pre_rstd = sem("pre_rstd"); pre_normed = sem("pre_normed")
        x_turned = sem("x_turned"); xt_low_made = sem("xt_low_made"); xt_hi_made = sem("xt_hi_made")
        xt_lo_made = sem("xt_lo_made")
        k_done = sem("k_done"); k_hi_made = sem("k_hi_made"); k_lo_made = sem("k_lo_made")
        v_done = sem("v_done"); v_hi_made = sem("v_hi_made"); v_lo_made = sem("v_lo_made")
        q_done = sem("q_done"); q_hi_made = sem("q_hi_made"); q_lo_made = sem("q_lo_made")
        s_done = sem("s_done"); s_copied = sem("s_copied"); max_made = sem("max_made"); exp_made = sem("exp_made")
        p_turned = sem("p_turned"); pt_hi_made = sem("pt_hi_made"); pt_lo_made = sem("pt_lo_made")
        pv_done = sem("pv_done"); y_hi_made = sem("y_hi_made"); y_lo_made = sem("y_lo_made")
        sum_made = sem("sum_made"); inv_made = sem("inv_made"); o_done = sem("o_done"); att_made = sem("att_made")
        stats = sem("stats"); moments = sem("moments"); eps_added = sem("eps_added"); rstd_made = sem("rstd_made")
        att_normed = sem("att_normed"); res_made = sem("res_made"); mix_in_made = sem("mix_in_made")
        mix_in_turned = sem("mix_in_turned"); xt_made = sem("xt_made"); carried = sem("carried")
        prev_part = sem("prev_part"); mixed_made = sem("mixed_made"); xm_hi_made = sem("xm_hi_made")
        xm_lo_made = sem("xm_lo_made")
        key_done = sem("key_done"); relu_made = sem("relu_made"); sq_made = sem("sq_made")
        sq_hi_made = sem("sq_hi_made"); sq_lo_made = sem("sq_lo_made")
        rec_done = sem("rec_done"); rec_exp = sem("rec_exp"); rec_plus = sem("rec_plus"); rec_made = sem("rec_made")
        val_done = sem("val_done"); f_made = sem("f_made"); f_normed = sem("f_normed"); out_made = sem("out_made")
        waited = sem("waited")
        EXPS = NT + 1

        stage_low = probs[:, 0, 0:3 * D]
        stage_mid = probs[:, 0, 3 * D:6 * D]
        stage_w = probs[:, 1, :].rearrange("p (w h c) -> p w h c", w=4, h=HALVES)

        PREP = S + T01 + M
        KPER = NJ * HALVES
        VPER = NKT // 2

        def key_bank(i, m):
            return PREP[(i * HALVES + m) % len(PREP)]

        QUERY_BANKS = [PREP[(KPER + m) % len(PREP)] for m in range(HALVES)]

        def value_bank(n):
            return PREP[(KPER + HALVES + n) % len(PREP)]

        block = ctx.enter_context(nc.Block())

        @block.sync
        def _(sp):
            def load_x(b, i):
                n = x_in[i % 2]
                sp.dma_start(xin[:, i % 2, :, 0:LOW], xb[b, i, :, :, D - LOW:D]).then_inc(n, 16)
                sp.dma_start(xin[:, i % 2, :, LOW:2 * LOW], xb[b, i, :, :, 0:LOW]).then_inc(n, 16)
                sp.dma_start(xin[:, i % 2, :, 2 * LOW:D], xb[b, i, :, :, LOW:D - LOW]).then_inc(n, 16)

            def load_x_late(b):
                for i in range(2, PRE):
                    sp.wait_ge(x_turned, b * PRE + i - 1)
                    load_x(b, i)

            def store(b, j, following):
                sp.wait_ge(out_made, (b * NJ + j + 1) * NT)
                if following is not None:
                    sp.dma_start(res[:, :, :], xb[following]).then_inc(res_in, 16)
                sp.dma_start(ob[b, j], att[:, :, :]).then_inc(stored, 16)
                sp.wait_ge(stored, (b * NJ + j + 1) * 16)
                sp.sem_inc(att_free, 1)

            load_x(0, 0)
            load_x(0, 1)
            sp.dma_start(stage_low[0:LOW, :], w_qkv[D - LOW:D, :]).then_inc(w_in, 16)
            sp.dma_start(stage_low[LOW:P, :], w_qkv[0:LOW, :]).then_inc(w_in, 16)
            sp.dma_start(stage_mid, w_qkv[LOW:D - LOW, :]).then_inc(w_in, 16)
            for i, w in ((OUT, out_w), (KEY, w_k), (REC, w_r), (VAL, w_v)):
                sp.dma_start(stage_w[:, i], w.rearrange("(h p) c -> p h c", p=P)).then_inc(w_in, 16)
            sp.dma_start(bias_row[:, :], out_b.rearrange("(a n) -> a n", a=1).broadcast_to([P, D])).then_inc(vec_in, 16)
            for i, m in enumerate((mu_k, mu_r)):
                for h in range(HALVES):
                    sp.dma_start(mu[:, i, h:h + 1], m[h * P:(h + 1) * P].rearrange("(p a) -> p a", a=1)).then_inc(vec_in, 16)
            sp.dma_start(res[:, :, :], xb[0, 0]).then_inc(res_in, 16)
            sp.sem_inc(att_free, 1)
            load_x_late(0)
            with sp.Fori(0, NB - 1) as b:
                sp.wait_ge(x_turned, (b + 1) * PRE)
                load_x(b + 1, 0)
                load_x(b + 1, 1)
                with sp.Fori(0, NJ - 2) as j:
                    store(b, j, (b, j + 1))
                load_x_late(b + 1)
                store(b, NJ - 2, (b, NJ - 1))
                store(b, NJ - 1, (b + 1, 0))
            with sp.Fori(0, NJ - 2) as j:
                store(NB - 1, j, (NB - 1, j + 1))
            store(NB - 1, NJ - 2, (NB - 1, NJ - 1))
            store(NB - 1, NJ - 1, None)

        @block.gpsimd
        def _(pool):
            pool.memset(ident[:, :], 0.0).then_inc(ident_zero, 1)
            pool.memset(minus_half[:, :], -0.5).then_inc(consts_made, 1)
            pool.memset(eps[:, :], EPS).then_inc(consts_made, 1)
            pool.wait_ge(ident_zero, 1)
            pool.affine_select(out=ident[:, :], in_=ident[:, :], compare_op=ALU.not_equal, fill=1.0, base=0,
                               pattern=[[-1, P]], channel_multiplier=1).then_inc(ident_made, 1)
            pool.wait_ge(consts_made, 2)

            def rsqrt(g3):
                pool.wait_ge(moments, (g3 + 1) * NT)
                pool.tensor_tensor(var_eps[:, :], mv[:, :, 1], eps[:, :], ALU.add).then_inc(eps_added, 1)
                pool.wait_ge(eps_added, g3 + 1)
                pool.tensor_tensor(rstd[:, :], var_eps[:, :], minus_half[:, :], ALU.pow).then_inc(rstd_made, 1)

            def pre_rsqrt(n):
                pool.wait_ge(pre_moments, (n + 1) * NT)
                pool.tensor_tensor(pvar_eps[:, :], pmv[:, :, 1], eps[:, :], ALU.add).then_inc(pre_eps, 1)
                pool.wait_ge(pre_eps, n + 1)
                pool.tensor_tensor(prstd[:, :], pvar_eps[:, :], minus_half[:, :], ALU.pow).then_inc(pre_rstd, 1)

            def split_low(g, i):
                for h in range(HALVES):
                    n = 2 * i + h
                    pool.wait_ge(xm_hi_made, g * 4 + n + 1)
                    pool.tensor_tensor(xm_lo[:, h, :], mixed[:, h, :], f32(xm_hi[:, h, :]),
                                       ALU.subtract).then_inc(xm_lo_made, 1)

            def post_first(g, turn):
                if turn is not None:
                    pre_rsqrt(turn * PRE)
                pool.wait_ge(res_in, (g + 1) * 16)
                rsqrt(g * 3)
                for t in range(NT):
                    pool.wait_ge(att_normed, g * NT + t + 1)
                    pool.tensor_tensor(res[:, t, :], res[:, t, :], att[:, t, :], ALU.add).then_inc(res_made, 1)
                if turn is not None:
                    pre_rsqrt(turn * PRE + 1)
                rsqrt(g * 3 + 1)
                split_low(g, 0)

            def post_second(g, turn, first_next):
                if turn is not None:
                    pre_rsqrt(turn * PRE + 2)
                split_low(g, 1)
                if first_next:
                    pool.memset(xt[:, :, 0:1], 0.0).then_inc(carried, 1)
                else:
                    pool.tensor_copy(xt[:, :, 0:1], xt[:, :, BLK:BLK + 1]).then_inc(carried, 1)
                for m in range(HALVES):
                    pool.wait_ge(sq_hi_made, g * 2 + m + 1)
                    pool.tensor_tensor(yk_lo[:, m, :], mixed[:, m, :], f32(yk_hi[:, m, :]),
                                       ALU.subtract).then_inc(sq_lo_made, 1)
                if turn is not None:
                    pre_rsqrt(turn * PRE + 3)
                rsqrt(g * 3 + 2)
                for t in range(NT):
                    pool.wait_ge(f_normed, g * NT + t + 1)
                    pool.tensor_tensor(att[:, t, :], att[:, t, :], res[:, t, :], ALU.add).then_inc(out_made, 1)

            for i in range(PRE):
                pre_rsqrt(i)
            pool.memset(xt[:, :, 0:1], 0.0).then_inc(carried, 1)

            def steady(b):
                with pool.Fori(0, NJ - 2) as j:
                    post_first(b * NJ + j, None)
                    post_second(b * NJ + j, None, False)

            with pool.Fori(0, NB - 1) as b:
                steady(b)
                post_first(b * NJ + NJ - 2, b + 1)
                post_second(b * NJ + NJ - 2, b + 1, False)
                post_first(b * NJ + NJ - 1, None)
                post_second(b * NJ + NJ - 1, None, True)
            steady(NB - 1)
            post_first(NB * NJ - 2, None)
            post_second(NB * NJ - 2, None, False)
            post_first(NB * NJ - 1, None)
            post_second(NB * NJ - 1, None, True)

        @block.scalar
        def _(act):
            def copy(out_, in_):
                return act.activation(out_, in_, ACT.Copy)

            def x_out(n, i, banks):
                cols = slice(i * BLK, (i + 1) * BLK)
                act.wait_ge(x_turned, n + 1)
                copy(xt_low[:, cols], banks[0][:, :]).then_inc(xt_low_made, 1)
                copy(xt_hi[:, cols], banks[1][:, :]).then_inc(xt_hi_made, 1)

            def keys_out(b, i):
                for m in range(HALVES):
                    act.wait_ge(k_done, (b * PRE + i) * HALVES + m + 1)
                    copy(k_hi[:, m, i * BLK:(i + 1) * BLK], key_bank(i, m)[:, :]).then_inc(k_hi_made, 1)

            def values_out(b):
                for n in range(VPER):
                    act.wait_ge(v_done, b * VPER + n + 1)
                    copy(v_hi[:, 2 * n:2 * n + 2, :], pair(value_bank(n)[:, :])).then_inc(v_hi_made, 1)

            def queries_out(g, banks):
                for m in range(HALVES):
                    act.wait_ge(q_done, g * HALVES + m + 1)
                    copy(q_hi[:, m, :], banks[m][:, :]).then_inc(q_hi_made, 1)

            def softmax_exp(g, t):
                act.wait_ge(max_made, g * NT + t + 1)
                if t < NT - 1:
                    act.activation(probs[:, t, :], probs[:, t, :], ACT.Exp, bias=neg_max[:, t:t + 1], scale=SCALE,
                                   accum_out=row_sum[:, t:t + 1]).then_inc(exp_made, 1)
                else:
                    for n, cols in enumerate((slice(0, BLK), slice(BLK, N))):
                        act.activation(probs[:, t, cols], probs[:, t, cols], ACT.Exp, bias=neg_max[:, t:t + 1],
                                       scale=SCALE, accum_out=part_sum[:, n:n + 1]).then_inc(exp_made, 1)

            def before(g, i):
                for h in range(HALVES):
                    act.wait_ge(xt_made, g * 2 + h + 1)
                    if i == 1:
                        act.wait_ge(mixed_made, g * 4 + h + 1)
                    act.activation(tmp[:, h, :], xt[:, h, 0:BLK], ACT.Copy,
                                   scale=one_minus_mu[:, i, h:h + 1]).then_inc(prev_part, 1)

            def split_high(g, i):
                for h in range(HALVES):
                    act.wait_ge(mixed_made, g * 4 + 2 * i + h + 1)
                    if i == 1:
                        act.wait_ge(key_done, g * 2 + 2)
                    copy(xm_hi[:, h, :], mixed[:, h, :]).then_inc(xm_hi_made, 1)

            def score_stage(g, post, turn):
                if post:
                    p = g - 1
                    act.wait_ge(pv_done, (p + 1) * NKT)
                    for m in range(HALVES):
                        copy(yk_hi[:, m, :], Y[m][:, :]).then_inc(y_hi_made, 1)
                softmax_exp(g, 0)
                softmax_exp(g, 1)
                if turn is not None:
                    x_out(turn * PRE, 0, T01)
                softmax_exp(g, 2)
                if turn is not None:
                    x_out(turn * PRE + 1, 1, T01)
                if post:
                    post_turned(p)
                softmax_exp(g, 3)

            def post_turned(p):
                act.wait_ge(carried, p + 1)
                for h in range(HALVES):
                    act.wait_ge(mix_in_turned, p * 2 + h + 1)
                    copy(xt[:, h, 1:BLK + 1], M[h][:, :]).then_inc(xt_made, 1)
                before(p, 0)
                split_high(p, 0)

            def relu(p):
                act.wait_ge(mixed_made, p * 4 + 4)
                for m in range(HALVES):
                    act.wait_ge(key_done, p * 2 + m + 1)
                    act.activation(tmp[:, m, :], M[m][:, :], ACT.Relu).then_inc(relu_made, 1)

            def square_high(p):
                for m in range(HALVES):
                    act.wait_ge(sq_made, p * 2 + m + 1)
                    copy(yk_hi[:, m, :], mixed[:, m, :]).then_inc(sq_hi_made, 1)

            def receptance(p):
                for i in range(2):
                    act.wait_ge(rec_done, p * 2 + i + 1)
                    act.activation(tmp[:, i, :], M[i][:, :], ACT.Exp, scale=-1.0).then_inc(rec_exp, 1)

            def value_stage(g, post, turn, queries):
                p = g - 1
                for kt in range(NKT):
                    act.wait_ge(p_turned, g * NKT + kt + 1)
                    if kt >= RING:
                        act.wait_ge(pv_done, g * NKT + kt - RING + 1)
                    copy(pt_hi[:, kt % RING, :], T[kt % 4][:, :]).then_inc(pt_hi_made, 1)
                    if post:
                        if kt == 0:
                            before(p, 1)
                        if kt == 1:
                            relu(p)
                        if kt == 2:
                            split_high(p, 1)
                        if kt == 5:
                            square_high(p)
                        if kt == 6:
                            receptance(p)
                    if turn is not None:
                        if kt == 8:
                            x_out(turn * PRE + 2, 2, M)
                        if kt == 13:
                            x_out(turn * PRE + 3, 3, M)
                    if queries and kt == 14:
                        queries_out(g + 1, M)

            def prepare(b, first):
                for i in range(PRE):
                    if first and i + 1 < PRE:
                        x_out(i + 1, i + 1, Y)
                    keys_out(b, i)
                queries_out(b * NJ, QUERY_BANKS)
                values_out(b)

            act.wait_ge(mu_made, 1)
            act.wait_ge(w_in, 7 * 16)
            copy(wq_low[:, :], stage_low).then_inc(w_hi_made, 1)
            copy(wq_hi[:, :], stage_mid).then_inc(w_hi_made, 1)
            for i in range(4):
                act.wait_ge(w_turned, i + 1)
                copy(wt_hi[:, i], (S + M)[i][:, :]).then_inc(w_hi_made, 1)
            x_out(0, 0, Y)
            prepare(0, True)
            score_stage(0, False, None)
            value_stage(0, False, None, True)

            def steady(b):
                with act.Fori(0, NJ - 2) as j:
                    score_stage(b * NJ + j + 1, True, None)
                    value_stage(b * NJ + j + 1, True, None, True)

            with act.Fori(0, NB - 1) as b:
                steady(b)
                score_stage(b * NJ + NJ - 1, True, b + 1)
                value_stage(b * NJ + NJ - 1, True, b + 1, False)
                prepare(b + 1, False)
                score_stage(b * NJ + NJ, True, None)
                value_stage(b * NJ + NJ, True, None, True)
            steady(NB - 1)
            last = NB * NJ - 1
            score_stage(last, True, None)
            value_stage(last, True, None, False)
            act.wait_ge(pv_done, (last + 1) * NKT)
            for m in range(HALVES):
                copy(yk_hi[:, m, :], Y[m][:, :]).then_inc(y_hi_made, 1)
            post_turned(last)
            before(last, 1)
            relu(last)
            split_high(last, 1)
            square_high(last)
            receptance(last)

        @block.vector
        def _(dve):
            def low_part(out_lo, psum, hi):
                return dve.tensor_tensor(out_lo, psum, f32(hi), ALU.subtract)

            def pre_stat(n):
                dve.wait_ge(x_in[n_parity(n)], n_half(n) * 48)
                for t in range(NT):
                    dve.bn_stats(pst[:, t, :], xin[:, n_parity(n), t, :]).then_inc(pre_stats, 1)
                dve.wait_ge(pre_stats, n_all(n) * NT + NT)
                dve.sem_inc(waited, 1)
                for t in range(NT):
                    dve.bn_aggr(pmv[:, t, :], pst[:, t, :]).then_inc(pre_moments, 1)

            def n_parity(n):
                return n[1] % 2

            def n_half(n):
                return n[0] * (PRE // 2) + n[1] // 2 + 1

            def n_all(n):
                return n[0] * PRE + n[1]

            def pre_norm(n):
                dve.wait_ge(pre_rstd, n_all(n) + 1)
                for t in range(NT):
                    o = xin[:, n_parity(n), t, :]
                    dve.tensor_scalar(o, o, pmv[:, t, 0:1], prstd[:, t:t + 1],
                                      ALU.subtract, ALU.mult).then_inc(pre_normed, 1)

            def x_low(n, banks):
                cols = slice(n[1] * BLK, (n[1] + 1) * BLK)
                dve.wait_ge(xt_hi_made, n_all(n) + 1)
                low_part(xt_lo[:, cols], banks[1][:, :], xt_hi[:, cols]).then_inc(xt_lo_made, 1)

            def keys_low(n):
                for m in range(HALVES):
                    cols = slice(n[1] * BLK, (n[1] + 1) * BLK)
                    dve.wait_ge(k_hi_made, n_all(n) * HALVES + m + 1)
                    low_part(k_lo[:, m, cols], key_bank(n[1], m)[:, :], k_hi[:, m, cols]).then_inc(k_lo_made, 1)

            def values_low(b):
                for n in range(VPER):
                    o = slice(2 * n, 2 * n + 2)
                    dve.wait_ge(v_hi_made, b * VPER + n + 1)
                    low_part(v_lo[:, o, :], pair(value_bank(n)[:, :]), v_hi[:, o, :]).then_inc(v_lo_made, 1)

            def queries_low(g, banks):
                for m in range(HALVES):
                    dve.wait_ge(q_hi_made, g * HALVES + m + 1)
                    low_part(q_lo[:, m, :], banks[m][:, :], q_hi[:, m, :]).then_inc(q_lo_made, 1)

            def score_out(g, u):
                t, c = divmod(u, NC)
                dve.wait_ge(s_done, g * UNITS + u + 1)
                dve.tensor_scalar(probs[:, t, c * BLK:(c + 1) * BLK], S[u % 2][:, :], 1.0, None, ALU.mult, ALU.max,
                                  accum_out=chunk_max[:, t, c:c + 1]).then_inc(s_copied, 1)
                if c == NC - 1:
                    dve.wait_ge(s_copied, g * UNITS + u + 1)
                    dve.tensor_scalar(scaled_max[:, t, :], chunk_max[:, t, :], -SCALE, None, ALU.mult, ALU.min,
                                      accum_out=neg_max[:, t:t + 1]).then_inc(max_made, 1)

            def tile_stats(src, t):
                dve.bn_stats(st[:, t, :], src[:, t, :]).then_inc(stats, 1)

            def tile_moments(n3):
                dve.wait_ge(stats, (n3 + 1) * NT)
                dve.sem_inc(waited, 1)
                for t in range(NT):
                    dve.bn_aggr(mv[:, t, :], st[:, t, :]).then_inc(moments, 1)

            def y_low(p, m):
                dve.wait_ge(y_hi_made, p * 2 + m + 1)
                low_part(yk_lo[:, m, :], Y[m][:, :], yk_hi[:, m, :]).then_inc(y_lo_made, 1)

            def inverse_sums(p):
                dve.wait_ge(exp_made, (p + 1) * EXPS)
                dve.tensor_scalar(sum_copy[:, :], part_sum[:, :], 1.0, None, ALU.mult, ALU.add,
                                  accum_out=row_sum[:, NT - 1:NT]).then_inc(sum_made, 1)
                dve.wait_ge(sum_made, p + 1)
                dve.reciprocal(inv_sum[:, :], row_sum[:, :]).then_inc(inv_made, 1)

            def attention(p, t):
                dve.wait_ge(o_done, p * 2 + t // 2 + 1)
                dve.wait_ge(att_free, p + 1)
                dve.wait_ge(inv_made, p + 1)
                dve.scalar_tensor_tensor(out=att[:, t, :], in0=M[t // 2][:, (t % 2) * D:(t % 2 + 1) * D],
                                         scalar=inv_sum[:, t:t + 1], in1=bias_row[:, :],
                                         op0=ALU.mult, op1=ALU.add).then_inc(att_made, 1)

            def attention_stat(p, t):
                dve.wait_ge(att_made, p * NT + t + 1)
                tile_stats(att, t)

            def attention_norm(p):
                dve.wait_ge(rstd_made, p * 3 + 1)
                for t in range(NT):
                    dve.tensor_scalar(att[:, t, :], att[:, t, :], mv[:, t, 0:1], rstd[:, t:t + 1],
                                      ALU.subtract, ALU.mult).then_inc(att_normed, 1)

            def res_stat(p, t):
                dve.wait_ge(res_made, p * NT + t + 1)
                tile_stats(res, t)

            def mix_in(p):
                dve.wait_ge(rstd_made, p * 3 + 2)
                for t in range(NT):
                    dve.tensor_scalar(att[:, t, :], res[:, t, :], mv[:, t, 0:1], rstd[:, t:t + 1],
                                      ALU.subtract, ALU.mult).then_inc(mix_in_made, 1)

            def mixes(p, i):
                for h in range(HALVES):
                    n = 2 * i + h
                    dve.wait_ge(prev_part, p * 4 + n + 1)
                    if i == 1:
                        dve.wait_ge(xm_lo_made, p * 4 + h + 1)
                    dve.scalar_tensor_tensor(out=mixed[:, h, :], in0=xt[:, h, 1:BLK + 1], scalar=mu[:, i, h:h + 1],
                                             in1=tmp[:, h, :], op0=ALU.mult, op1=ALU.add).then_inc(mixed_made, 1)

            def squares(p):
                for m in range(HALVES):
                    dve.wait_ge(relu_made, p * 2 + m + 1)
                    dve.wait_ge(xm_lo_made, p * 4 + 3 + m)
                    dve.tensor_tensor(mixed[:, m, :], M[m][:, :], tmp[:, m, :], ALU.mult).then_inc(sq_made, 1)

            def one_plus(p):
                for i in range(2):
                    dve.wait_ge(rec_exp, p * 2 + i + 1)
                    dve.tensor_scalar(tmp[:, i, :], tmp[:, i, :], 1.0, None, ALU.add).then_inc(rec_plus, 1)

            def sigmoid(p, t):
                i, cols = t // 2, slice((t % 2) * D, (t % 2 + 1) * D)
                dve.wait_ge(rec_plus, p * 2 + i + 1)
                dve.reciprocal(tmp[:, i, cols], tmp[:, i, cols]).then_inc(rec_made, 1)

            def gated(p):
                for i in range(2):
                    dve.wait_ge(val_done, p * 2 + i + 1)
                    dve.wait_ge(rec_made, p * NT + 2 * i + 2)
                    dve.tensor_tensor(att[:, 2 * i:2 * i + 2, :], pair(M[i][:, :]), pair(tmp[:, i, :]),
                                      ALU.mult).then_inc(f_made, 1)

            def gated_stats(p):
                for t in range(NT):
                    dve.wait_ge(f_made, p * 2 + t // 2 + 1)
                    tile_stats(att, t)
                tile_moments(p * 3 + 2)

            def gated_norm(p):
                dve.wait_ge(rstd_made, p * 3 + 3)
                for t in range(NT):
                    dve.tensor_scalar(att[:, t, :], att[:, t, :], mv[:, t, 0:1], rstd[:, t:t + 1],
                                      ALU.subtract, ALU.mult).then_inc(f_normed, 1)

            def score_stage(g, post, turn):
                p = g - 1
                for u in range(UNITS):
                    score_out(g, u)
                    if post:
                        if u == 0:
                            y_low(p, 0)
                            y_low(p, 1)
                            inverse_sums(p)
                        if u == 2:
                            attention(p, 0)
                            attention(p, 1)
                        if u == 3:
                            attention(p, 2)
                            attention(p, 3)
                            attention_stat(p, 0)
                        if u == 4:
                            attention_stat(p, 1)
                            attention_stat(p, 2)
                        if u == 5:
                            attention_stat(p, 3)
                            tile_moments(p * 3)
                        if u == 7:
                            attention_norm(p)
                        if u == 8:
                            res_stat(p, 0)
                            res_stat(p, 1)
                        if u == 9:
                            res_stat(p, 2)
                            res_stat(p, 3)
                            tile_moments(p * 3 + 1)
                        if u == 11:
                            mix_in(p)
                        if u == 13:
                            mixes(p, 0)
                    if turn is not None:
                        if u == 1:
                            pre_stat((turn, 0))
                        if u == 4:
                            pre_norm((turn, 0))
                        if u == 6:
                            pre_stat((turn, 1))
                        if u == 8:
                            x_low((turn, 0), T01)
                        if u == 10:
                            pre_norm((turn, 1))
                        if u == 12:
                            x_low((turn, 1), T01)

            def value_stage(g, post, turn, queries):
                p = g - 1
                for kt in range(NKT):
                    dve.wait_ge(pt_hi_made, g * NKT + kt + 1)
                    low_part(pt_lo[:, kt % RING, :], T[kt % 4][:, :], pt_hi[:, kt % RING, :]).then_inc(pt_lo_made, 1)
                    if post:
                        if kt == 0:
                            mixes(p, 1)
                        if kt == 4:
                            squares(p)
                        if kt == 6:
                            one_plus(p)
                        if 7 <= kt < 7 + NT:
                            sigmoid(p, kt - 7)
                        if kt == 11:
                            gated(p)
                        if kt == 12:
                            gated_stats(p)
                        if kt == 14:
                            gated_norm(p)
                    if turn is not None:
                        if kt == 1:
                            pre_stat((turn, 2))
                        if kt == 3:
                            pre_norm((turn, 2))
                        if kt == 5:
                            pre_stat((turn, 3))
                        if kt == 8:
                            x_low((turn, 2), M)
                        if kt == 9:
                            pre_norm((turn, 3))
                        if kt == 13:
                            x_low((turn, 3), M)
                    if queries and kt == 14:
                        queries_low(g + 1, M)

            def prepare(b, first):
                for i in range(PRE):
                    if first and i + 1 < PRE:
                        pre_norm((b, i + 1))
                        if i + 2 < PRE:
                            pre_stat((b, i + 2))
                        x_low((b, i + 1), Y)
                    keys_low((b, i))
                queries_low(b * NJ, QUERY_BANKS)
                values_low(b)

            dve.wait_ge(vec_in, (1 + 2 * HALVES) * 16)
            dve.tensor_scalar(one_minus_mu[:, :, :], mu[:, :, :], -1.0, 1.0, ALU.mult, ALU.add).then_inc(mu_made, 1)
            pre_stat((0, 0))
            dve.wait_ge(w_hi_made, 2)
            low_part(wq_lo[:, :], stage_mid, wq_hi[:, :]).then_inc(w_lo_made, 1)
            for i in range(4):
                dve.wait_ge(w_hi_made, 3 + i)
                low_part(wt_lo[:, i], (S + M)[i][:, :].rearrange("p (h d) -> p h d", h=HALVES),
                         wt_hi[:, i]).then_inc(w_lo_made, 1)
            pre_norm((0, 0))
            pre_stat((0, 1))
            x_low((0, 0), Y)
            prepare(0, True)
            score_stage(0, False, None)
            value_stage(0, False, None, True)

            def steady(b):
                with dve.Fori(0, NJ - 2) as j:
                    score_stage(b * NJ + j + 1, True, None)
                    value_stage(b * NJ + j + 1, True, None, True)

            with dve.Fori(0, NB - 1) as b:
                steady(b)
                score_stage(b * NJ + NJ - 1, True, b + 1)
                value_stage(b * NJ + NJ - 1, True, b + 1, False)
                prepare(b + 1, False)
                score_stage(b * NJ + NJ, True, None)
                value_stage(b * NJ + NJ, True, None, True)
            steady(NB - 1)
            last = NB * NJ - 1
            score_stage(last, True, None)
            value_stage(last, True, None, False)
            y_low(last, 0)
            y_low(last, 1)
            inverse_sums(last)
            for t in range(NT):
                attention(last, t)
            for t in range(NT):
                attention_stat(last, t)
            tile_moments(last * 3)
            attention_norm(last)
            for t in range(NT):
                res_stat(last, t)
            tile_moments(last * 3 + 1)
            mix_in(last)
            mixes(last, 0)
            mixes(last, 1)
            squares(last)
            one_plus(last)
            for t in range(NT):
                sigmoid(last, t)
            gated(last)
            gated_stats(last)
            gated_norm(last)

        @block.tensor
        def _(pe):
            def three(out_, a_hi, a_lo, b_hi, b_lo, start, stop):
                pe.matmul(out_, a_hi, b_hi, start=start, stop=False)
                pe.matmul(out_, a_hi, b_lo, start=False, stop=False)
                return pe.matmul(out_, a_lo, b_hi, start=False, stop=stop)

            def turn_x(n, i, banks):
                pe.wait_ge(pre_normed, (n + 1) * NT)
                for t in range(NT):
                    for band in range(2):
                        mm = pe.transpose(banks[band][:, t * P:(t + 1) * P],
                                          xin[:, i % 2, t, band * P:(band + 1) * P], ident[:, :])
                mm.then_inc(x_turned, 1)

            def project(out_, w_cols, x_cols):
                pe.matmul(out_, wq_low[:, w_cols], xt_low[:, x_cols], start=True, stop=False)
                return three(out_, wq_hi[:, w_cols], wq_lo[:, w_cols], xt_hi[:, x_cols], xt_lo[:, x_cols], False, True)

            def bank_taken_out(b, n):
                if n < 0:
                    return
                if n < KPER:
                    pe.wait_ge(k_lo_made, b * KPER + n + 1)
                elif n < KPER + HALVES:
                    pe.wait_ge(q_lo_made, b * (NJ * HALVES) + n - KPER + 1)
                else:
                    pe.wait_ge(v_lo_made, b * VPER + n - KPER - HALVES + 1)

            def keys(b, i):
                pe.wait_ge(xt_low_made, b * PRE + i + 1)
                pe.wait_ge(xt_lo_made, b * PRE + i + 1)
                for m in range(HALVES):
                    bank_taken_out(b, i * HALVES + m - len(PREP))
                    project(key_bank(i, m)[:, :], slice(D + m * P, D + (m + 1) * P), slice(i * BLK, (i + 1) * BLK)).then_inc(k_done, 1)

            def queries(j, banks):
                for m in range(HALVES):
                    project(banks[m][:, :], slice(m * P, (m + 1) * P), bass.ds(j * BLK, BLK)).then_inc(q_done, 1)

            def values(b):
                for n in range(VPER):
                    bank_taken_out(b, KPER + HALVES + n - len(PREP))
                    for i in range(2):
                        t = 2 * n + i
                        rows, cols = slice(t * P, (t + 1) * P), slice(2 * D, 3 * D)
                        o = value_bank(n)[:, i * D:(i + 1) * D]
                        pe.matmul(o, xt_low[:, rows], wq_low[:, cols], start=True, stop=False)
                        mm = three(o, xt_hi[:, rows], xt_lo[:, rows], wq_hi[:, cols], wq_lo[:, cols], False, True)
                    mm.then_inc(v_done, 1)

            def scores(g, u):
                t, c = divmod(u, NC)
                if u >= 2:
                    pe.wait_ge(s_copied, g * UNITS + u - 1)
                rows, cols = slice(t * P, (t + 1) * P), slice(c * BLK, (c + 1) * BLK)
                for m in range(HALVES):
                    mm = three(S[u % 2][:, :], q_hi[:, m, rows], q_lo[:, m, rows], k_hi[:, m, cols], k_lo[:, m, cols],
                               m == 0, m == HALVES - 1)
                mm.then_inc(s_done, 1)

            def turn_probs(g, kt):
                if kt == 0:
                    pe.wait_ge(exp_made, g * EXPS + NT)
                if kt == NC:
                    pe.wait_ge(exp_made, (g + 1) * EXPS)
                for t in range(NT):
                    mm = pe.transpose(T[kt % 4][:, t * P:(t + 1) * P], probs[:, t, kt * P:(kt + 1) * P], ident[:, :])
                mm.then_inc(p_turned, 1)

            def by_rows(a_hi, a_lo, w, done):
                for t in range(NT):
                    rows = slice(t * P, (t + 1) * P)
                    for h in range(HALVES):
                        mm = three(M[t // 2][:, (t % 2) * D:(t % 2 + 1) * D], a_hi[:, h, rows], a_lo[:, h, rows],
                                   wt_hi[:, w, h, :], wt_lo[:, w, h, :], h == 0, h == HALVES - 1)
                    if t % 2:
                        mm.then_inc(done, 1)

            def project_out(p):
                pe.wait_ge(y_lo_made, p * 2 + 2)
                by_rows(yk_hi, yk_lo, OUT, o_done)

            def turn_mix_in(p):
                pe.wait_ge(mix_in_made, p * NT + NT)
                for h in range(HALVES):
                    for t in range(NT):
                        mm = pe.transpose(M[h][:, t * P:(t + 1) * P], att[:, t, h * P:(h + 1) * P], ident[:, :])
                    mm.then_inc(mix_in_turned, 1)

            def mix_keys(p):
                pe.wait_ge(xm_lo_made, p * 4 + 2)
                for m in range(HALVES):
                    cols = slice(m * P, (m + 1) * P)
                    for h in range(HALVES):
                        mm = three(M[m][:, :], wt_hi[:, KEY, h, cols], wt_lo[:, KEY, h, cols], xm_hi[:, h, :],
                                   xm_lo[:, h, :], h == 0, h == HALVES - 1)
                    mm.then_inc(key_done, 1)

            def receptance(p):
                pe.wait_ge(xm_lo_made, p * 4 + 4)
                pe.wait_ge(sq_made, p * 2 + 2)
                by_rows(xm_hi, xm_lo, REC, rec_done)

            def mix_values(p):
                pe.wait_ge(sq_lo_made, p * 2 + 2)
                pe.wait_ge(rec_exp, p * 2 + 2)
                by_rows(yk_hi, yk_lo, VAL, val_done)

            def score_stage(g, post, turn):
                p = g - 1
                pe.wait_ge(q_lo_made, (g + 1) * HALVES)
                for u in range(UNITS):
                    scores(g, u)
                    if post:
                        if u == 1:
                            project_out(p)
                        if u == 12:
                            turn_mix_in(p)
                    if turn is not None:
                        if u == 7:
                            turn_x(turn * PRE, 0, T01)
                        if u == 11:
                            pe.wait_ge(xt_lo_made, turn * PRE + 1)
                            turn_x(turn * PRE + 1, 1, T01)
                if post:
                    mix_keys(p)

            def value_stage(g, post, turn, next_block):
                p = g - 1
                if turn is not None:
                    pe.wait_ge(xt_lo_made, turn * PRE + 2)
                for kt in range(3):
                    turn_probs(g, kt)
                for kt in range(NKT):
                    pe.wait_ge(pt_lo_made, g * NKT + kt + 1)
                    s = kt % RING
                    for m in range(HALVES):
                        cols = slice(m * P, (m + 1) * P)
                        mm = three(Y[m][:, :], v_hi[:, kt, cols], v_lo[:, kt, cols], pt_hi[:, s, :], pt_lo[:, s, :],
                                   kt == 0, kt == NKT - 1)
                    mm.then_inc(pv_done, 1)
                    if kt + 3 < NKT:
                        turn_probs(g, kt + 3)
                    if turn is not None:
                        if kt == 7:
                            pe.wait_ge(rec_exp, p * 2 + 2)
                            turn_x(turn * PRE + 2, 2, M)
                        if kt == 9:
                            pe.wait_ge(xt_lo_made, turn * PRE + 3)
                        if kt == 12:
                            pe.wait_ge(f_made, p * 2 + 2)
                            turn_x(turn * PRE + 3, 3, M)
                    if post:
                        if kt == 5:
                            receptance(p)
                        if kt == 9:
                            mix_values(p)
                    if next_block is not None and kt == 13:
                        if post:
                            pe.wait_ge(f_made, p * 2 + 2)
                        queries(next_block, M)

            def prepare(b, first):
                for i in range(PRE):
                    if first and i + 1 < PRE:
                        pe.wait_ge(xt_lo_made, i + 1)
                        turn_x(i + 1, i + 1, Y)
                    keys(b, i)
                bank_taken_out(b, KPER + HALVES - 1 - len(PREP))
                queries(0, QUERY_BANKS)
                values(b)
                pe.wait_ge(v_lo_made, b * VPER + VPER - len(PREP) + len(S))

            pe.wait_ge(w_in, 7 * 16)
            pe.wait_ge(ident_made, 1)
            for i in range(4):
                for h in range(HALVES):
                    for e in range(HALVES):
                        mm = pe.transpose((S + M)[i][:, h * D + e * P:h * D + (e + 1) * P],
                                          stage_w[:, i, e, h * P:(h + 1) * P], ident[:, :])
                mm.then_inc(w_turned, 1)
            turn_x(0, 0, Y)
            pe.wait_ge(w_lo_made, 5)
            prepare(0, True)
            score_stage(0, False, None)
            value_stage(0, False, None, 1)

            def steady(b):
                with pe.Fori(0, NJ - 2) as j:
                    score_stage(b * NJ + j + 1, True, None)
                    value_stage(b * NJ + j + 1, True, None, j + 2)

            with pe.Fori(0, NB - 1) as b:
                steady(b)
                score_stage(b * NJ + NJ - 1, True, b + 1)
                value_stage(b * NJ + NJ - 1, True, b + 1, None)
                prepare(b + 1, False)
                score_stage(b * NJ + NJ, True, None)
                value_stage(b * NJ + NJ, True, None, 1)
            steady(NB - 1)
            last = NB * NJ - 1
            score_stage(last, True, None)
            value_stage(last, True, None, None)
            project_out(last)
            turn_mix_in(last)
            mix_keys(last)
            receptance(last)
            mix_values(last)


_INS = ["L0_attn_x", "L0_attn_weight_qkv", "L0_attn_out_w", "L0_attn_out_b", "L0_ffn_W_r", "L0_ffn_W_k",
        "L0_ffn_W_v", "L0_ffn_mu_r", "L0_ffn_mu_k"]


def kernel(**inputs):
    import numpy as np
    import concourse.bacc as bacc
    from concourse.bass_utils import run_bass_kernel_spmd

    nc = bacc.Bacc("TRN2", target_bir_lowering=False, num_devices=1)
    arrays, args = {}, []
    for name in _INS:
        a = np.ascontiguousarray(inputs[name])
        arrays[f"in_{name}"] = a
        args.append(nc.dram_tensor(f"in_{name}", a.shape, mybir.dt.from_np(a.dtype), kind="ExternalInput").ap())
    shape = arrays["in_L0_attn_x"].shape
    out = nc.dram_tensor("out_x", shape, F32, kind="ExternalOutput").ap()
    sandwich(nc, *args, out)
    r = run_bass_kernel_spmd(nc, [arrays], core_ids=[0])
    return r.results[0]["out_x"]
```

```python
from contextlib import ExitStack

import concourse.bass as bass
from concourse import mybir

F32 = mybir.dt.float32
F32R = mybir.dt.float32r
F16 = mybir.dt.float16
ALU = mybir.AluOpType
ACT = mybir.ActivationFunctionType

P = 128
BLK = 512
EPS = 1e-5


def sandwich(nc, x, w_qkv, out_w, out_b, w_r, w_k, w_v, mu_r, mu_k, out):
    NB, N, D = x.shape
    LOW = D // 4
    HALVES = D // P
    NJ = N // BLK
    NT = BLK // P
    NC = N // BLK
    NKT = N // P
    UNITS = NT * NC
    SCALE = float(D) ** -0.5
    RING = 4
    AHEAD = 3
    XPER = 2
    assert D == 2 * P and N % BLK == 0 and NJ == XPER * (NJ - 2)

    xb = x.rearrange("b (j t p) d -> b j p t d", p=P, t=NT)
    ob = out.rearrange("b (j t p) d -> b j p t d", p=P, t=NT)

    ctx = ExitStack()
    with ctx:
        def sb(name, shape, dt=F32):
            return ctx.enter_context(nc.sbuf_tensor(name, shape, dt))

        def sem(name):
            return ctx.enter_context(nc.semaphore(name))

        def bank(name):
            return ctx.enter_context(nc.psum_tensor(name, [P, BLK], F32))

        ident = sb("ident", [P, P])
        QK, OUT, KEY, REC, VAL = range(5)
        wt_hi = sb("wt_hi", [P, 5, HALVES, D], F32R)
        wt_lo = sb("wt_lo", [P, 5, HALVES, D], F32R)
        w_half = sb("w_half", [P, 3 * D], F16)
        bias_row = sb("bias_row", [P, D])
        mu = sb("mu", [P, 2, HALVES])
        minus_half = sb("minus_half", [P, NT])
        eps = sb("eps", [P, NT])
        zeros = sb("zeros", [P, NT])

        xin = sb("xin", [P, NJ, NT, D])
        x_half = sb("x_half", [P, NT, P], F16)
        xt_low = sb("xt_low", [P, N], F32R)
        xt_hi = sb("xt_hi", [P, N], F32R)
        xt_lo = sb("xt_lo", [P, N], F32R)
        v_hi = sb("v_hi", [P, NKT, D], F32R)
        v_lo = sb("v_lo", [P, NKT, P], F32R)
        pst = sb("pst", [P, NJ, NT, 6])
        pmv = sb("pmv", [P, NJ, NT, 2])
        pvar_eps = sb("pvar_eps", [P, NJ, NT])
        prstd = sb("prstd", [P, NJ, NT])

        q_hi = sb("q_hi", [P, HALVES, BLK], F32R)
        q_lo = sb("q_lo", [P, HALVES, BLK], F32R)
        probs = sb("probs", [P, NT, N])
        chunk_max = sb("chunk_max", [P, NT, NC])
        scaled_max = sb("scaled_max", [P, NT, NC])
        neg_max = sb("neg_max", [P, NT])
        part_sum = sb("part_sum", [P, 2])
        sum_copy = sb("sum_copy", [P, 2])
        row_sum = sb("row_sum", [P, NT])
        inv_sum = sb("inv_sum", [P, NT])
        pt_hi = sb("pt_hi", [P, RING, BLK], F32R)
        pt_lo = sb("pt_lo", [P, RING, BLK], F32R)
        x_res = sb("x_res", [P, NT, D])
        res = sb("res", [P, NT, D])
        att = sb("att", [P, NT, D])
        gate = sb("gate", [P, NT, D])
        st = sb("st", [P, NT, 6])
        mv = sb("mv", [P, NT, 2])
        var_eps = sb("var_eps", [P, NT])
        rstd = sb("rstd", [P, NT])
        minus_mean = sb("minus_mean", [P, NT])
        shift = sb("shift", [P, NT])
        gst = sb("gst", [P, NT, 6])
        gmv = sb("gmv", [P, NT, 2])
        gvar_eps = sb("gvar_eps", [P, NT])
        grstd = sb("grstd", [P, NT])
        gminus_mean = sb("gminus_mean", [P, NT])
        gshift = sb("gshift", [P, NT])
        xt = sb("xt", [P, HALVES, BLK + 1])
        tmp = sb("tmp", [P, 2, HALVES, BLK])
        mixed = sb("mixed", [P, 2, HALVES, BLK])
        xm_hi = sb("xm_hi", [P, 2, HALVES, BLK], F32R)
        xm_lo = sb("xm_lo", [P, 2, HALVES, BLK], F32R)
        yk_hi = sb("yk_hi", [P, HALVES, BLK], F32R)
        yk_lo = sb("yk_lo", [P, HALVES, BLK], F32R)

        S = [bank(f"S{i}") for i in range(4)]
        T = S[2:] + S[:2]
        Y = [bank(f"Y{i}") for i in range(HALVES)]
        M = [bank(f"M{i}") for i in range(2)]

        def unit(u, first):
            if first is not None and u < 2 * NC:
                return u % 2, u // 2
            return divmod(u, NC)

        def f32(ap):
            return ap.bitcast(F32)

        def pair(ap):
            return ap.rearrange("p (t d) -> p t d", t=2)

        qk_in = sem("qk_in"); vo_in = sem("vo_in"); w_in = sem("w_in"); vec_in = sem("vec_in")
        ident_zero = sem("ident_zero"); ident_made = sem("ident_made"); consts_made = sem("consts_made")
        w_half_made = sem("w_half_made"); w_rounded = sem("w_rounded"); w_turned = sem("w_turned")
        w_copied = sem("w_copied"); w_multiplied = sem("w_multiplied")
        w_hi_made = sem("w_hi_made"); w_lo_made = sem("w_lo_made")
        x_in = [sem(f"x_in{i}") for i in range(NJ)]
        pre_stats = sem("pre_stats"); pre_moments = sem("pre_moments"); pre_eps = sem("pre_eps")
        pre_rstd = sem("pre_rstd"); pre_normed = sem("pre_normed"); x_half_made = sem("x_half_made")
        xn_made = sem("xn_made"); x_turned = sem("x_turned"); xt_low_made = sem("xt_low_made")
        xt_hi_made = sem("xt_hi_made"); xt_lo_made = sem("xt_lo_made")
        v_hi_made = sem("v_hi_made"); v_lo_made = sem("v_lo_made")
        q_done = sem("q_done"); q_hi_made = sem("q_hi_made"); q_lo_made = sem("q_lo_made")
        s_done = sem("s_done"); s_copied = sem("s_copied"); max_made = sem("max_made"); exp_made = sem("exp_made")
        p_turned = sem("p_turned"); pt_hi_made = sem("pt_hi_made"); pt_lo_made = sem("pt_lo_made")
        pv_done = sem("pv_done"); y_hi_made = sem("y_hi_made"); y_lo_made = sem("y_lo_made")
        sum_made = sem("sum_made"); inv_made = sem("inv_made"); o_done = sem("o_done"); att_made = sem("att_made")
        res_in = sem("res_in"); stored = sem("stored")
        stats = sem("stats"); moments = sem("moments"); eps_added = sem("eps_added"); mean_turned = sem("mean_turned")
        rstd_made = sem("rstd_made"); shift_made = sem("shift_made")
        att_normed = sem("att_normed"); res_made = sem("res_made"); mix_in_made = sem("mix_in_made")
        mix_in_turned = sem("mix_in_turned"); xt_made = sem("xt_made"); carried = sem("carried")
        diff_made = sem("diff_made"); mixed_made = sem("mixed_made"); xm_hi_made = sem("xm_hi_made")
        xm_lo_made = sem("xm_lo_made")
        key_done = sem("key_done"); relu_made = sem("relu_made"); sq_made = sem("sq_made"); sq_hi_made = sem("sq_hi_made")
        sq_lo_made = sem("sq_lo_made")
        rec_done = sem("rec_done"); rec_exp = sem("rec_exp"); rec_plus = sem("rec_plus"); rec_made = sem("rec_made")
        val_done = sem("val_done"); gated_made = sem("gated_made")
        g_stats = sem("g_stats"); g_moments = sem("g_moments"); g_eps_added = sem("g_eps_added")
        g_mean_turned = sem("g_mean_turned"); g_rstd_made = sem("g_rstd_made"); g_shift_made = sem("g_shift_made")
        g_normed = sem("g_normed"); out_made = sem("out_made")
        waited = sem("waited")
        EXPS = NT + 1

        stage_qkv = [probs[:, 0, h * 3 * D:(h + 1) * 3 * D] for h in range(HALVES)]
        stage_w = tmp.rearrange("p i h c -> p (i h c)").rearrange("p (w h c) -> p w h c", w=4, h=HALVES)
        QK_COLS, V_COLS = slice(0, 2 * D), slice(2 * D, 3 * D)
        STAGED = (out_w, w_k, w_r, w_v)
        turned_w = mixed.rearrange("p i h c -> p (i h c)").rearrange("p (w h c) -> p w h c", w=4, h=HALVES)
        W_BANKS = S + Y[1:] + M
        QK_BANK, OUT_BANK = Y[1], S[0]
        SPLIT = ((QK, QK_BANK), (OUT, OUT_BANK), (KEY, W_BANKS[4]), (REC, W_BANKS[5]), (VAL, W_BANKS[6]))

        last = NB * NJ - 1
        PT = NT // 2
        last_res = probs[:, 0, 0:NT * D].rearrange("p (t d) -> p t d", t=NT)
        last_rec = probs[:, 1, 0:2 * BLK].rearrange("p (i c) -> p i c", i=2)
        HALF = PT * P
        STEPS = NKT // 2
        A_STEP = STEPS + 2

        def half_tiles(a):
            return range(a * PT, (a + 1) * PT)

        def half_cols(a):
            return slice(a * PT * P, (a + 1) * PT * P)

        block = ctx.enter_context(nc.Block())

        @block.sync
        def _(sp):
            def load_x(b, i):
                n = x_in[i]
                sp.dma_start(xin[:, i, :, 0:LOW], xb[b, i, :, :, D - LOW:D]).then_inc(n, 16)
                sp.dma_start(xin[:, i, :, LOW:2 * LOW], xb[b, i, :, :, 0:LOW]).then_inc(n, 16)
                sp.dma_start(xin[:, i, :, 2 * LOW:D], xb[b, i, :, :, LOW:D - LOW]).then_inc(n, 16)

            def block_io(g, at, following):
                sp.wait_ge(res_made, (g + 1) * NT)
                sp.dma_start(x_res[:, :, :], xb[following]).then_inc(res_in, 16)
                sp.wait_ge(out_made, (g + 1) * NT)
                sp.dma_start(ob[at], gate[:, :, :]).then_inc(stored, 16)

            def load_qkv(cols, done):
                sp.dma_start(stage_qkv[0][0:LOW, cols], w_qkv[D - LOW:D, cols]).then_inc(done, 16)
                sp.dma_start(stage_qkv[0][LOW:P, cols], w_qkv[0:LOW, cols]).then_inc(done, 16)
                sp.dma_start(stage_qkv[1][:, cols], w_qkv[LOW:D - LOW, cols]).then_inc(done, 16)

            load_qkv(QK_COLS, qk_in)
            load_x(0, 0)
            load_x(0, 1)
            load_qkv(V_COLS, vo_in)
            for i, w in enumerate(STAGED):
                sp.dma_start(stage_w[:, i], w.rearrange("(h p) c -> p h c", p=P)).then_inc(vo_in if i == 0 else w_in, 16)
                if i < NJ - 2:
                    load_x(0, i + 2)
            sp.dma_start(bias_row[:, :], out_b.rearrange("(a n) -> a n", a=1).broadcast_to([P, D])).then_inc(vec_in, 16)
            for i, m in enumerate((mu_r, mu_k)):
                for h in range(HALVES):
                    sp.dma_start(mu[:, i, h:h + 1], m[h * P:(h + 1) * P].rearrange("(p a) -> p a", a=1)).then_inc(vec_in, 16)
            sp.dma_start(x_res[:, :, :], xb[0, 0]).then_inc(res_in, 16)
            with sp.Fori(0, NB - 1) as b:
                sp.wait_ge(x_turned, (b + 1) * NJ)
                sp.wait_ge(v_lo_made, (b + 1) * NJ)
                for i in range(NJ):
                    load_x(b + 1, i)
                with sp.Fori(0, NJ - 1) as j:
                    block_io(b * NJ + j, (b, j), (b, j + 1))
                block_io(b * NJ + NJ - 1, (b, NJ - 1), (b + 1, 0))
            with sp.Fori(0, NJ - 1) as j:
                block_io((NB - 1) * NJ + j, (NB - 1, j), (NB - 1, j + 1))
            for a in range(2):
                tiles = slice(a * PT, (a + 1) * PT)
                sp.wait_ge(out_made, last * NT + (a + 1) * PT)
                sp.dma_start(ob[NB - 1, NJ - 1][:, tiles, :], gate[:, tiles, :]).then_inc(stored, 16)
            sp.wait_ge(stored, (NB * NJ + 1) * 16)

        @block.gpsimd
        def _(pool):
            pool.memset(ident[:, :], 0.0).then_inc(ident_zero, 1)
            pool.memset(minus_half[:, :], -0.5).then_inc(consts_made, 1)
            pool.memset(eps[:, :], EPS).then_inc(consts_made, 1)
            pool.memset(zeros[:, :], 0.0).then_inc(consts_made, 1)
            pool.wait_ge(ident_zero, 1)
            pool.affine_select(out=ident[:, :], in_=ident[:, :], compare_op=ALU.not_equal, fill=1.0, base=0,
                               pattern=[[-1, P]], channel_multiplier=1).then_inc(ident_made, 1)
            pool.wait_ge(consts_made, 3)

            def rsqrt(p, i):
                n = p * 2 + i
                pool.wait_ge(moments, (n + 1) * NT)
                pool.tensor_tensor(var_eps[:, :], mv[:, :, 1], eps[:, :], ALU.add).then_inc(eps_added, 1)
                if i == 0:
                    pool.tensor_tensor(minus_mean[:, :], zeros[:, :], mv[:, :, 0], ALU.subtract).then_inc(mean_turned, 1)
                pool.wait_ge(eps_added, n + 1)
                pool.tensor_tensor(rstd[:, :], var_eps[:, :], minus_half[:, :], ALU.pow).then_inc(rstd_made, 1)
                if i == 0:
                    pool.wait_ge(rstd_made, n + 1)
                    pool.wait_ge(mean_turned, p + 1)
                    pool.tensor_tensor(shift[:, :], minus_mean[:, :], rstd[:, :], ALU.mult).then_inc(shift_made, 1)

            def gate_rsqrt(p):
                pool.wait_ge(g_moments, (p + 1) * NT)
                pool.tensor_tensor(gvar_eps[:, :], gmv[:, :, 1], eps[:, :], ALU.add).then_inc(g_eps_added, 1)
                pool.tensor_tensor(gminus_mean[:, :], zeros[:, :], gmv[:, :, 0], ALU.subtract).then_inc(g_mean_turned, 1)
                pool.wait_ge(g_eps_added, p + 1)
                pool.tensor_tensor(grstd[:, :], gvar_eps[:, :], minus_half[:, :], ALU.pow).then_inc(g_rstd_made, 1)
                pool.wait_ge(g_rstd_made, p + 1)
                pool.wait_ge(g_mean_turned, p + 1)
                pool.tensor_tensor(gshift[:, :], gminus_mean[:, :], grstd[:, :], ALU.mult).then_inc(g_shift_made, 1)

            def pre_rsqrt(n, i):
                pool.wait_ge(pre_moments, (n + 1) * NT)
                pool.tensor_tensor(pvar_eps[:, i, :], pmv[:, i, :, 1], eps[:, :], ALU.add).then_inc(pre_eps, 1)
                pool.wait_ge(pre_eps, n + 1)
                pool.tensor_tensor(prstd[:, i, :], pvar_eps[:, i, :], minus_half[:, :], ALU.pow).then_inc(pre_rstd, 1)

            def split_low(p, i):
                for h in range(HALVES):
                    pool.wait_ge(xm_hi_made, p * 4 + 2 * i + h + 1)
                    pool.tensor_tensor(xm_lo[:, i, h, :], mixed[:, i, h, :], f32(xm_hi[:, i, h, :]),
                                       ALU.subtract).then_inc(xm_lo_made, 1)

            def differences(p):
                for h in range(HALVES):
                    pool.wait_ge(xt_made, p * 2 + h + 1)
                    pool.tensor_tensor(tmp[:, 0, h, :], xt[:, h, 1:BLK + 1], xt[:, h, 0:BLK],
                                       ALU.subtract).then_inc(diff_made, 1)

            def values_low(b, blocks):
                for i in blocks:
                    tiles = slice(i * NT, (i + 1) * NT)
                    pool.wait_ge(v_hi_made, b * NJ + i + 1)
                    pool.tensor_tensor(v_lo[:, tiles, :], xin[:, i, :, P:D], f32(v_hi[:, tiles, P:D]),
                                       ALU.subtract).then_inc(v_lo_made, 1)

            def finish(p):
                gate_rsqrt(p)
                add_residual(p)

            def add_residual(p):
                for t in range(NT):
                    pool.wait_ge(g_normed, p * NT + t + 1)
                    pool.tensor_tensor(gate[:, t, :], gate[:, t, :], res[:, t, :], ALU.add).then_inc(out_made, 1)

            def add_attention(p):
                pool.wait_ge(res_in, (p + 1) * 16)
                rsqrt(p, 0)
                for t in range(NT):
                    pool.wait_ge(att_normed, p * NT + t + 1)
                    pool.tensor_tensor(res[:, t, :], x_res[:, t, :], att[:, t, :], ALU.add).then_inc(res_made, 1)
                rsqrt(p, 1)

            def score_stage(g, post, older, first):
                if first is not None:
                    values_low(first, range(0, NJ // 2))
                if older:
                    finish(g - 2)
                if post:
                    add_attention(g - 1)
                if first is not None:
                    values_low(first, range(NJ // 2, NJ))

            def carry(p, next_first):
                if next_first:
                    pool.memset(xt[:, :, 0:1], 0.0).then_inc(carried, 1)
                else:
                    pool.tensor_copy(xt[:, :, 0:1], xt[:, :, BLK:BLK + 1]).then_inc(carried, 1)

            def value_stage(g, post, next_x, next_first):
                p = g - 1
                if post:
                    differences(p)
                if next_x is not None:
                    pre_rsqrt(next_x[0] * NJ + next_x[1], next_x[1])
                if post:
                    split_low(p, 0)
                    split_low(p, 1)
                if next_x is not None:
                    pre_rsqrt(next_x[0] * NJ + next_x[1] + 1, next_x[1] + 1)
                if post:
                    carry(p, next_first)
                    for m in range(HALVES):
                        pool.wait_ge(sq_made, p * 2 + m + 1)
                        pool.wait_ge(sq_hi_made, p * 2 + m + 1)
                        pool.tensor_tensor(yk_lo[:, m, :], mixed[:, 1, m, :], f32(yk_hi[:, m, :]),
                                           ALU.subtract).then_inc(sq_lo_made, 1)

            for i in range(NJ):
                pre_rsqrt(i, i)
            pool.memset(xt[:, :, 0:1], 0.0).then_inc(carried, 1)
            score_stage(0, False, False, 0)
            value_stage(0, False, None, False)
            score_stage(1, True, False, None)
            value_stage(1, True, None, False)
            with pool.Fori(0, NB - 1) as b:
                for j in range(2, NJ):
                    score_stage(b * NJ + j, True, True, None)
                    value_stage(b * NJ + j, True, (b + 1, (j - 2) * XPER), False)
                score_stage(b * NJ + NJ, True, True, b + 1)
                value_stage(b * NJ + NJ, True, None, True)
                score_stage(b * NJ + NJ + 1, True, True, None)
                value_stage(b * NJ + NJ + 1, True, None, False)
            for g in range((NB - 1) * NJ + 2, NB * NJ):
                score_stage(g, True, True, None)
                value_stage(g, True, None, False)

            def half_rsqrt(i, a):
                n = last * 2 + 2 * a + i + 1
                t = slice(a * PT, (a + 1) * PT)
                pool.wait_ge(moments, last * 2 * NT + (2 * a + i + 1) * PT)
                pool.tensor_tensor(var_eps[:, t], mv[:, t, 1], eps[:, t], ALU.add).then_inc(eps_added, 1)
                if (i, a) == (0, 0):
                    pool.tensor_tensor(minus_mean[:, t], zeros[:, t], mv[:, t, 0], ALU.subtract).then_inc(mean_turned, 1)
                pool.wait_ge(eps_added, n)
                pool.tensor_tensor(rstd[:, t], var_eps[:, t], minus_half[:, t], ALU.pow).then_inc(rstd_made, 1)
                if (i, a) == (0, 0):
                    pool.wait_ge(rstd_made, n)
                    pool.wait_ge(mean_turned, last + 1)
                    pool.tensor_tensor(shift[:, t], minus_mean[:, t], rstd[:, t], ALU.mult).then_inc(shift_made, 1)

            def half_gate_rsqrt(a):
                n = last + a + 1
                t = slice(a * PT, (a + 1) * PT)
                pool.wait_ge(g_moments, last * NT + (a + 1) * PT)
                pool.tensor_tensor(gvar_eps[:, t], gmv[:, t, 1], eps[:, t], ALU.add).then_inc(g_eps_added, 1)
                if a == 0:
                    pool.tensor_tensor(gminus_mean[:, t], zeros[:, t], gmv[:, t, 0], ALU.subtract).then_inc(g_mean_turned, 1)
                pool.wait_ge(g_eps_added, n)
                pool.tensor_tensor(grstd[:, t], gvar_eps[:, t], minus_half[:, t], ALU.pow).then_inc(g_rstd_made, 1)
                if a == 0:
                    pool.wait_ge(g_rstd_made, n)
                    pool.wait_ge(g_mean_turned, n)
                    pool.tensor_tensor(gshift[:, t], gminus_mean[:, t], grstd[:, t], ALU.mult).then_inc(g_shift_made, 1)

            half_rsqrt(0, 0)
            half_rsqrt(1, 0)
            half_rsqrt(0, 1)
            gate_rsqrt(last - 1)
            half_rsqrt(1, 1)
            for a in range(2):
                c = half_cols(a)
                for i in range(2):
                    for h in range(HALVES):
                        pool.wait_ge(xm_hi_made, last * 4 + a * 4 + i * 2 + h + 1)
                        pool.tensor_tensor(xm_lo[:, i, h, c], mixed[:, i, h, c], f32(xm_hi[:, i, h, c]),
                                           ALU.subtract).then_inc(xm_lo_made, 1)
            for a in range(2):
                c = half_cols(a)
                for m in range(HALVES):
                    pool.wait_ge(sq_made, last * 2 + a * 2 + m + 1)
                    pool.wait_ge(sq_hi_made, last * 2 + a * 2 + m + 1)
                    pool.tensor_tensor(yk_lo[:, m, c], mixed[:, 1, m, c], f32(yk_hi[:, m, c]),
                                       ALU.subtract).then_inc(sq_lo_made, 1)
            for a in range(2):
                half_gate_rsqrt(a)

        @block.scalar
        def _(act):
            def copy(out_, in_):
                return act.activation(out_, in_, ACT.Copy)

            def round_low(n, i, again=True):
                act.wait_ge(pre_normed, (n + 1) * NT)
                if again:
                    act.wait_ge(xn_made, n)
                copy(x_half[:, :, :], xin[:, i, :, 0:P]).then_inc(x_half_made, 1)
                act.wait_ge(x_half_made, n + 1)
                copy(xin[:, i, :, 0:P], x_half[:, :, :]).then_inc(xn_made, 1)

            def x_out_low(n, i, banks):
                act.wait_ge(x_turned, n + 1)
                copy(xt_low[:, i * BLK:(i + 1) * BLK], banks[0][:, :]).then_inc(xt_low_made, 1)

            def x_out_high(i, banks):
                copy(xt_hi[:, i * BLK:(i + 1) * BLK], banks[1][:, :]).then_inc(xt_hi_made, 1)

            def x_out(n, i, banks):
                x_out_low(n, i, banks)
                x_out_high(i, banks)

            def query_out(g, m, banks):
                act.wait_ge(q_done, g * HALVES + m + 1)
                copy(q_hi[:, m, :], banks[m][:, :]).then_inc(q_hi_made, 1)

            def queries_out(g, banks):
                for m in range(HALVES):
                    query_out(g, m, banks)

            def attention_out(p):
                act.wait_ge(pv_done, (p + 1) * NKT)
                for m in range(HALVES):
                    copy(yk_hi[:, m, :], Y[m][:, :]).then_inc(y_hi_made, 1)

            def next_batch(b):
                attention_out(b * NJ - 1)
                queries_out(b * NJ, M)
                x_out(b * NJ + 1, 1, S[2:])

            def softmax_exp(g, t, cols, total):
                act.wait_ge(max_made, g * NT + t + 1)
                act.activation(probs[:, t, cols], probs[:, t, cols], ACT.Exp, bias=neg_max[:, t:t + 1], scale=SCALE,
                               accum_out=total).then_inc(exp_made, 1)

            def row_exp(g, t):
                softmax_exp(g, t, slice(0, N), row_sum[:, t:t + 1])

            def gate_norm(p):
                act.wait_ge(g_shift_made, p + 1)
                for t in range(NT):
                    act.activation(gate[:, t, :], gate[:, t, :], ACT.Identity, bias=gshift[:, t:t + 1],
                                   scale=grstd[:, t:t + 1]).then_inc(g_normed, 1)

            def attention_norm(p):
                act.wait_ge(shift_made, p + 1)
                for t in range(NT):
                    act.activation(att[:, t, :], att[:, t, :], ACT.Identity, bias=shift[:, t:t + 1],
                                   scale=rstd[:, t:t + 1]).then_inc(att_normed, 1)

            def split_high(p, i, h):
                act.wait_ge(mixed_made, p * 4 + 2 * i + h + 1)
                copy(xm_hi[:, i, h, :], mixed[:, i, h, :]).then_inc(xm_hi_made, 1)

            def mix_in_out(p):
                act.wait_ge(carried, p + 1)
                for h in range(HALVES):
                    act.wait_ge(mix_in_turned, p * 2 + h + 1)
                    copy(xt[:, h, 1:BLK + 1], M[h][:, :]).then_inc(xt_made, 1)

            def relu(p):
                for m in range(HALVES):
                    act.wait_ge(key_done, p * 2 + m + 1)
                    act.activation(tmp[:, 1, m, :], M[m][:, :], ACT.Relu).then_inc(relu_made, 1)

            def squares(p):
                act.wait_ge(xm_lo_made, p * 4 + 4)
                for m in range(HALVES):
                    act.wait_ge(relu_made, p * 2 + m + 1)
                    act.activation(mixed[:, 1, m, :], tmp[:, 1, m, :], ACT.Square).then_inc(sq_made, 1)
                    act.activation(yk_hi[:, m, :], tmp[:, 1, m, :], ACT.Square).then_inc(sq_hi_made, 1)

            def receptance(p):
                act.wait_ge(mixed_made, p * 4 + 4)
                for i in range(2):
                    act.wait_ge(rec_done, p * 2 + i + 1)
                    act.activation(tmp[:, 0, i, :], M[i][:, :], ACT.Exp, scale=-1.0).then_inc(rec_exp, 1)

            def round_weights(i, cols, loaded, loads):
                act.wait_ge(loaded, loads * 16)
                copy(w_half[:, cols], stage_qkv[0][:, cols]).then_inc(w_half_made, 1)
                act.wait_ge(w_half_made, i + 1)
                copy(stage_qkv[0][:, cols], w_half[:, cols]).then_inc(w_rounded, 1)

            def weight_turned(i):
                act.wait_ge(w_turned, i + 1)
                copy(turned_w[:, i], pair(W_BANKS[i][:, :])).then_inc(w_copied, 1)

            def weight_high(i, produced, count):
                w, bank = SPLIT[i]
                act.wait_ge(produced, count)
                copy(wt_hi[:, w], pair(bank[:, :])).then_inc(w_hi_made, 1)

            def score_stage(g, post, older, first, halves=False):
                if post and first is None:
                    attention_out(g - 1)
                if first is not None:
                    x_out(first * NJ + 2, 2, Y)
                    if not post:
                        round_low(3, 3)
                        weight_high(1, w_multiplied, 2)
                    x_out(first * NJ + 3, 3, M)
                    if not post:
                        for i in range(2, len(SPLIT)):
                            weight_high(i, w_turned, 3 + i)
                if first is not None:
                    for i in range(NJ):
                        copy(v_hi[:, i * NT:(i + 1) * NT, :], xin[:, i, :, :]).then_inc(v_hi_made, 1)
                if older:
                    gate_norm(g - 2)
                for t in range(NT - 1):
                    if post and t == 1:
                        attention_norm(g - 1)
                    row_exp(g, t)
                if not halves:
                    softmax_exp(g, NT - 1, slice(0, BLK), part_sum[:, 0:1])

            def half_attention_out(a):
                act.wait_ge(pv_done, last * NKT + (a + 1) * STEPS)
                for m in range(HALVES):
                    copy(q_hi[:, m, half_cols(a)], Y[m][:, 0:HALF]).then_inc(y_hi_made, 1)

            def value_stage(g, post, next_x, next_query, next_b=None, halves=False):
                banks = S if halves else T
                p = g - 1
                if next_query:
                    query_out(g + 1, 0, S)
                if next_b is not None:
                    x_out_low(next_b * NJ, 0, S)
                for kt in range(NKT):
                    act.wait_ge(p_turned, g * NKT + kt + 1)
                    if kt >= RING:
                        act.wait_ge(pv_done, g * NKT + kt - RING + 1)
                    copy(pt_hi[:, kt % RING, :], banks[kt % 4][:, :]).then_inc(pt_hi_made, 1)
                    if halves and kt == A_STEP:
                        half_attention_out(0)
                    if kt == 0:
                        if next_query:
                            query_out(g + 1, 1, S)
                        if next_b is not None:
                            x_out_high(0, S)
                    if halves and kt == 1:
                        softmax_exp(g, NT - 1, slice(0, BLK), part_sum[:, 0:1])
                    if kt == (3 if halves else 1):
                        softmax_exp(g, NT - 1, slice(BLK, N), part_sum[:, 1:2])
                    if post:
                        if kt == 2:
                            mix_in_out(p)
                        if 4 <= kt < 8:
                            split_high(p, (kt - 4) // HALVES, kt % HALVES)
                        if kt == 9:
                            receptance(p)
                        if kt == 11:
                            relu(p)
                            squares(p)
                    if next_x is not None:
                        b, i = next_x
                        if kt == 12:
                            round_low(b * NJ + i, i)
                        if kt == 15:
                            round_low(b * NJ + i + 1, i + 1)

            round_weights(0, QK_COLS, qk_in, 3)
            weight_turned(0)
            weight_turned(1)
            round_weights(1, V_COLS, vo_in, 4)
            round_low(0, 0, again=False)
            weight_high(0, w_multiplied, 1)
            x_out(0, 0, S[:2])
            weight_turned(2)
            weight_turned(3)
            round_low(1, 1)
            queries_out(0, M)
            x_out(1, 1, S[2:])
            round_low(2, 2)
            score_stage(0, False, False, 0)
            value_stage(0, False, None, True)
            score_stage(1, True, False, None)
            value_stage(1, True, None, True)
            with act.Fori(0, NB - 1) as b:
                for j in range(2, NJ):
                    score_stage(b * NJ + j, True, True, None)
                    value_stage(b * NJ + j, True, (b + 1, (j - 2) * XPER), j + 1 < NJ, b + 1 if j + 1 == NJ else None)
                next_batch(b + 1)
                score_stage(b * NJ + NJ, True, True, b + 1)
                value_stage(b * NJ + NJ, True, None, True)
                score_stage(b * NJ + NJ + 1, True, True, None)
                value_stage(b * NJ + NJ + 1, True, None, True)
            score_stage(last - 1, True, True, None)
            value_stage(last - 1, True, None, True)
            score_stage(last, True, True, None, halves=True)
            value_stage(last, True, None, False, halves=True)
            half_attention_out(1)
            act.wait_ge(shift_made, last + 1)
            for t in half_tiles(0):
                act.activation(att[:, t, :], att[:, t, :], ACT.Identity, bias=shift[:, t:t + 1],
                               scale=rstd[:, t:t + 1]).then_inc(att_normed, 1)

            def half_mix_in_out(a):
                start = a * PT * P
                act.wait_ge(mix_in_turned, last * 2 + a + 1)
                for h in range(HALVES):
                    copy(xt[:, h, 1 + start:1 + start + PT * P], pair(Y[a][:, :])[:, h, :]).then_inc(xt_made, 1)

            def half_split_high(a, i):
                c = half_cols(a)
                for h in range(HALVES):
                    act.wait_ge(mixed_made, last * 4 + a * 4 + i * 2 + h + 1)
                    copy(xm_hi[:, i, h, c], mixed[:, i, h, c]).then_inc(xm_hi_made, 1)

            def half_squares(a):
                c = half_cols(a)
                act.wait_ge(key_done, last * 2 + a + 1)
                for m in range(HALVES):
                    act.activation(tmp[:, 1, m, c], pair(S[a][:, :])[:, m, :], ACT.Relu).then_inc(relu_made, 1)
                act.wait_ge(xm_lo_made, last * 4 + a * 4 + 4)
                for m in range(HALVES):
                    act.wait_ge(relu_made, last * 2 + a * 2 + m + 1)
                    act.activation(mixed[:, 1, m, c], tmp[:, 1, m, c], ACT.Square).then_inc(sq_made, 1)
                    act.activation(yk_hi[:, m, c], tmp[:, 1, m, c], ACT.Square).then_inc(sq_hi_made, 1)

            act.wait_ge(carried, last + 1)
            def half_receptance(a):
                act.wait_ge(rec_done, last * 2 + a + 1)
                act.activation(last_rec[:, a, :], S[2 + a][:, :], ACT.Exp, scale=-1.0).then_inc(rec_exp, 1)

            half_mix_in_out(0)
            gate_norm(last - 1)
            half_split_high(0, 0)
            half_split_high(0, 1)
            half_mix_in_out(1)
            half_split_high(1, 0)
            half_split_high(1, 1)
            half_receptance(0)
            half_squares(0)
            half_receptance(1)
            half_squares(1)
            act.wait_ge(g_shift_made, last + 1)
            for t in half_tiles(0):
                act.activation(gate[:, t, :], gate[:, t, :], ACT.Identity, bias=gshift[:, t:t + 1],
                               scale=grstd[:, t:t + 1]).then_inc(g_normed, 1)

        @block.vector
        def _(dve):
            def low_part(out_lo, psum, hi):
                return dve.tensor_tensor(out_lo, psum, f32(hi), ALU.subtract)

            def pre_stats_of(b, i, tiles=range(NT)):
                dve.wait_ge(x_in[i], (b + 1) * 48)
                for t in tiles:
                    dve.bn_stats(pst[:, i, t, :], xin[:, i, t, :]).then_inc(pre_stats, 1)

            def pre_moments_of(b, i):
                dve.wait_ge(pre_stats, (b * NJ + i + 1) * NT)
                dve.sem_inc(waited, 1)
                for t in range(NT):
                    dve.bn_aggr(pmv[:, i, t, :], pst[:, i, t, :]).then_inc(pre_moments, 1)

            def pre_stat(b, i):
                pre_stats_of(b, i)
                pre_moments_of(b, i)

            def pre_norm(b, i):
                dve.wait_ge(pre_rstd, b * NJ + i + 1)
                for t in range(NT):
                    o = xin[:, i, t, :]
                    dve.tensor_scalar(o, o, pmv[:, i, t, 0:1], prstd[:, i, t:t + 1],
                                      ALU.subtract, ALU.mult).then_inc(pre_normed, 1)

            def x_low(n, i, banks):
                cols = slice(i * BLK, (i + 1) * BLK)
                dve.wait_ge(xt_hi_made, n + 1)
                low_part(xt_lo[:, cols], banks[1][:, :], xt_hi[:, cols]).then_inc(xt_lo_made, 1)

            def queries_low(g, banks):
                for m in range(HALVES):
                    dve.wait_ge(q_hi_made, g * HALVES + m + 1)
                    low_part(q_lo[:, m, :], banks[m][:, :], q_hi[:, m, :]).then_inc(q_lo_made, 1)

            def next_batch(b):
                attention_low(b * NJ - 1)
                inverse_sums(b * NJ - 1)
                queries_low(b * NJ, M)
                x_low(b * NJ + 1, 1, S[2:])

            def score_out(g, u, first):
                t, c = unit(u, first)
                dve.wait_ge(s_done, g * UNITS + u + 1)
                dve.tensor_scalar(probs[:, t, c * BLK:(c + 1) * BLK], S[u % 4][:, :], 1.0, None, ALU.mult, ALU.max,
                                  accum_out=chunk_max[:, t, c:c + 1]).then_inc(s_copied, 1)
                if c == NC - 1:
                    dve.wait_ge(s_copied, g * UNITS + u + 1)
                    dve.tensor_scalar(scaled_max[:, t, :], chunk_max[:, t, :], -SCALE, None, ALU.mult, ALU.min,
                                      accum_out=neg_max[:, t:t + 1]).then_inc(max_made, 1)

            def attention_low(p):
                for m in range(HALVES):
                    dve.wait_ge(y_hi_made, p * 2 + m + 1)
                    low_part(yk_lo[:, m, :], Y[m][:, :], yk_hi[:, m, :]).then_inc(y_lo_made, 1)

            def inverse_sums(p):
                dve.wait_ge(exp_made, (p + 1) * EXPS)
                dve.tensor_scalar(sum_copy[:, :], part_sum[:, :], 1.0, None, ALU.mult, ALU.add,
                                  accum_out=row_sum[:, NT - 1:NT]).then_inc(sum_made, 1)
                dve.wait_ge(sum_made, p + 1)
                dve.reciprocal(inv_sum[:, :], row_sum[:, :]).then_inc(inv_made, 1)

            def attention(p, t):
                dve.wait_ge(o_done, p * 2 + t // 2 + 1)
                dve.wait_ge(inv_made, p + 1)
                dve.scalar_tensor_tensor(out=att[:, t, :], in0=M[t // 2][:, (t % 2) * D:(t % 2 + 1) * D],
                                         scalar=inv_sum[:, t:t + 1], in1=bias_row[:, :],
                                         op0=ALU.mult, op1=ALU.add).then_inc(att_made, 1)

            def tile_moments(p, i):
                dve.wait_ge(stats, (p * 2 + i + 1) * NT)
                dve.sem_inc(waited, 1)
                for t in range(NT):
                    dve.bn_aggr(mv[:, t, :], st[:, t, :]).then_inc(moments, 1)

            def attention_stat(p, t):
                dve.wait_ge(att_made, p * NT + t + 1)
                dve.bn_stats(st[:, t, :], att[:, t, :]).then_inc(stats, 1)

            def res_stat(p, t):
                dve.wait_ge(res_made, p * NT + t + 1)
                dve.bn_stats(st[:, t, :], res[:, t, :]).then_inc(stats, 1)

            def mix_in(p):
                dve.wait_ge(rstd_made, p * 2 + 2)
                for t in range(NT):
                    dve.tensor_scalar(att[:, t, :], res[:, t, :], mv[:, t, 0:1], rstd[:, t:t + 1],
                                      ALU.subtract, ALU.mult).then_inc(mix_in_made, 1)

            def mix(p, i, h):
                dve.wait_ge(diff_made, p * 2 + h + 1)
                dve.scalar_tensor_tensor(out=mixed[:, i, h, :], in0=tmp[:, 0, h, :], scalar=mu[:, i, h:h + 1],
                                         in1=xt[:, h, 0:BLK], op0=ALU.mult, op1=ALU.add).then_inc(mixed_made, 1)

            def one_plus(p):
                for i in range(2):
                    dve.wait_ge(rec_exp, p * 2 + i + 1)
                    dve.tensor_scalar(tmp[:, 0, i, :], tmp[:, 0, i, :], 1.0, None, ALU.add).then_inc(rec_plus, 1)

            def sigmoid(p, t):
                i, cols = t // 2, slice((t % 2) * D, (t % 2 + 1) * D)
                dve.wait_ge(rec_plus, p * 2 + i + 1)
                dve.reciprocal(tmp[:, 0, i, cols], tmp[:, 0, i, cols]).then_inc(rec_made, 1)

            def gated(p, older):
                for i in range(2):
                    dve.wait_ge(val_done, p * 2 + i + 1)
                    dve.wait_ge(rec_made, p * NT + 2 * i + 2)
                    if older:
                        dve.wait_ge(stored, p * 16)
                    dve.tensor_tensor(gate[:, 2 * i:2 * i + 2, :], pair(M[i][:, :]), pair(tmp[:, 0, i, :]),
                                      ALU.mult).then_inc(gated_made, 1)

            def gated_stats_of(p, tiles):
                for t in tiles:
                    dve.wait_ge(gated_made, p * 2 + t // 2 + 1)
                    dve.bn_stats(gst[:, t, :], gate[:, t, :]).then_inc(g_stats, 1)

            def gated_moments(p):
                dve.wait_ge(g_stats, (p + 1) * NT)
                dve.sem_inc(waited, 1)
                for t in range(NT):
                    dve.bn_aggr(gmv[:, t, :], gst[:, t, :]).then_inc(g_moments, 1)

            def weight_low(i):
                w, bank = SPLIT[i]
                dve.wait_ge(w_hi_made, i + 1)
                low_part(wt_lo[:, w], pair(bank[:, :]), wt_hi[:, w]).then_inc(w_lo_made, 1)

            def score_stage(g, post, older, first, halves=False):
                p = g - 1
                for u in range(UNITS):
                    score_out(g, u, first)
                    if first is not None:
                        if u == (0 if post else 2):
                            x_low(first * NJ + 2, 2, Y)
                        if u == 3 and not post:
                            weight_low(1)
                        if u == (1 if post else 3):
                            x_low(first * NJ + 3, 3, M)
                        if 8 <= u < 8 + len(SPLIT) - 2 and not post:
                            weight_low(u - 6)
                    if post:
                        if u == 0 and first is None:
                            attention_low(p)
                            inverse_sums(p)
                        if u == 1 and older:
                            gated_stats_of(p - 1, range(NT))
                            gated_moments(p - 1)
                        if u == 3:
                            attention(p, 0)
                            attention(p, 1)
                        if u == 4:
                            attention(p, 2)
                            attention(p, 3)
                            attention_stat(p, 0)
                        if u == 5:
                            attention_stat(p, 1)
                            attention_stat(p, 2)
                            attention_stat(p, 3)
                            tile_moments(p, 0)
                        if u == (10 if first is None else 11):
                            res_stat(p, 0)
                            res_stat(p, 1)
                        if u == (11 if first is None else 12):
                            res_stat(p, 2)
                            res_stat(p, 3)
                            tile_moments(p, 1)
                        if u == 15 and not halves:
                            mix_in(p)

            def half_attention_low(a):
                for m in range(HALVES):
                    dve.wait_ge(y_hi_made, last * HALVES + a * HALVES + m + 1)
                    low_part(q_lo[:, m, half_cols(a)], Y[m][:, 0:HALF], q_hi[:, m, half_cols(a)]).then_inc(y_lo_made, 1)

            def half_moments(i, a):
                dve.wait_ge(stats, last * 2 * NT + (2 * a + i + 1) * PT)
                dve.sem_inc(waited, 1)
                for t in half_tiles(a):
                    dve.bn_aggr(mv[:, t, :], st[:, t, :]).then_inc(moments, 1)

            def half_attention(a):
                for t in half_tiles(a):
                    attention(last, t)

            def half_attention_stats(a):
                for t in half_tiles(a):
                    dve.wait_ge(att_made, last * NT + t + 1)
                    dve.bn_stats(st[:, t, :], att[:, t, :]).then_inc(stats, 1)
                half_moments(0, a)

            def value_stage(g, post, older, next_x, next_query, next_b=None, halves=False):
                p = g - 1
                banks = S if halves else T
                for kt in range(NKT):
                    dve.wait_ge(pt_hi_made, g * NKT + kt + 1)
                    low_part(pt_lo[:, kt % RING, :], banks[kt % 4][:, :], pt_hi[:, kt % RING, :]).then_inc(pt_lo_made, 1)
                    if halves:
                        if kt == 0:
                            mix_in(p)
                        if kt == A_STEP:
                            half_attention_low(0)
                            inverse_sums(last)
                        if kt == A_STEP + 3:
                            half_attention(0)
                        if kt == A_STEP + 4:
                            half_attention_stats(0)
                    if kt == 0 and next_query:
                        queries_low(g + 1, S)
                    if kt == 0 and next_b is not None:
                        x_low(next_b * NJ, 0, S)
                    if post:
                        if 3 <= kt < 7:
                            mix(p, (kt - 3) // HALVES, (kt - 3) % HALVES)
                        if kt == 10:
                            one_plus(p)
                        if 10 <= kt < 10 + NT:
                            sigmoid(p, kt - 10)
                        if kt == 15:
                            gated(p, older)
                    if next_x is not None:
                        b, i = next_x
                        if kt in (1, 2):
                            pre_stats_of(b, i, range((kt - 1) * NT // 2, kt * NT // 2))
                        if kt == 3:
                            pre_moments_of(b, i)
                        if kt in (7, 8):
                            pre_stats_of(b, i + 1, range((kt - 7) * NT // 2, (kt - 6) * NT // 2))
                        if kt == 9:
                            pre_moments_of(b, i + 1)
                            pre_norm(b, i)
                        if kt == 14:
                            pre_norm(b, i + 1)

            pre_stat(0, 0)
            pre_norm(0, 0)
            pre_stat(0, 1)
            weight_low(0)
            pre_stats_of(0, 2)
            x_low(0, 0, S[:2])
            pre_norm(0, 1)
            pre_moments_of(0, 2)
            pre_stats_of(0, 3)
            queries_low(0, M)
            pre_norm(0, 2)
            pre_moments_of(0, 3)
            x_low(1, 1, S[2:])
            pre_norm(0, 3)
            dve.wait_ge(vec_in, (1 + 2 * HALVES) * 16)
            score_stage(0, False, False, 0)
            value_stage(0, False, False, None, True)
            score_stage(1, True, False, None)
            value_stage(1, True, False, None, True)
            with dve.Fori(0, NB - 1) as b:
                for j in range(2, NJ):
                    score_stage(b * NJ + j, True, True, None)
                    value_stage(b * NJ + j, True, True, (b + 1, (j - 2) * XPER), j + 1 < NJ,
                                b + 1 if j + 1 == NJ else None)
                next_batch(b + 1)
                score_stage(b * NJ + NJ, True, True, b + 1)
                value_stage(b * NJ + NJ, True, True, None, True)
                score_stage(b * NJ + NJ + 1, True, True, None)
                value_stage(b * NJ + NJ + 1, True, True, None, True)
            score_stage(last - 1, True, True, None)
            value_stage(last - 1, True, True, None, True)
            score_stage(last, True, True, None, halves=True)
            value_stage(last, True, True, None, False, halves=True)

            def half_residual(a):
                if a == 1:
                    dve.wait_ge(rstd_made, last * 2 + 3)
                    for t in half_tiles(a):
                        dve.tensor_scalar(att[:, t, :], att[:, t, :], mv[:, t, 0:1], rstd[:, t:t + 1],
                                          ALU.subtract, ALU.mult).then_inc(att_normed, 1)
                for t in half_tiles(a):
                    dve.wait_ge(att_normed, last * NT + t + 1)
                    dve.tensor_tensor(last_res[:, t, :], x_res[:, t, :], att[:, t, :], ALU.add).then_inc(res_made, 1)
                for t in half_tiles(a):
                    dve.wait_ge(res_made, last * NT + t + 1)
                    dve.bn_stats(st[:, t, :], last_res[:, t, :]).then_inc(stats, 1)
                half_moments(1, a)

            def half_mix_in(a):
                dve.wait_ge(rstd_made, last * 2 + 2 * a + 2)
                for t in half_tiles(a):
                    dve.tensor_scalar(att[:, t, :], last_res[:, t, :], mv[:, t, 0:1], rstd[:, t:t + 1],
                                      ALU.subtract, ALU.mult).then_inc(mix_in_made, 1)

            def half_differences(a):
                c = half_cols(a)
                for h in range(HALVES):
                    dve.wait_ge(xt_made, last * 2 + a * 2 + h + 1)
                    dve.tensor_tensor(tmp[:, 0, h, c], xt[:, h, 1 + c.start:1 + c.stop], xt[:, h, c],
                                      ALU.subtract).then_inc(diff_made, 1)

            def half_mix(a, i):
                c = half_cols(a)
                for h in range(HALVES):
                    dve.wait_ge(diff_made, last * 2 + a * 2 + h + 1)
                    dve.scalar_tensor_tensor(out=mixed[:, i, h, c], in0=tmp[:, 0, h, c], scalar=mu[:, i, h:h + 1],
                                             in1=xt[:, h, c], op0=ALU.mult, op1=ALU.add).then_inc(mixed_made, 1)

            def half_sigmoid(a, tiles):
                for t in tiles:
                    cols = slice((t % PT) * D, (t % PT + 1) * D)
                    dve.wait_ge(rec_plus, last * 2 + a + 1)
                    dve.reciprocal(last_rec[:, a, cols], last_rec[:, a, cols]).then_inc(rec_made, 1)

            def half_one_plus(a):
                dve.wait_ge(rec_exp, last * 2 + a + 1)
                dve.tensor_scalar(last_rec[:, a, :], last_rec[:, a, :], 1.0, None, ALU.add).then_inc(rec_plus, 1)

            def half_gated(a):
                dve.wait_ge(val_done, last * 2 + a + 1)
                dve.wait_ge(rec_made, last * NT + (a + 1) * PT)
                dve.tensor_tensor(gate[:, a * PT:(a + 1) * PT, :], pair(M[a][:, :]), pair(last_rec[:, a, :]),
                                  ALU.mult).then_inc(gated_made, 1)

            def half_gated_stats(a):
                dve.wait_ge(gated_made, last * 2 + a + 1)
                for t in half_tiles(a):
                    dve.bn_stats(gst[:, t, :], gate[:, t, :]).then_inc(g_stats, 1)
                dve.wait_ge(g_stats, last * NT + (a + 1) * PT)
                dve.sem_inc(waited, 1)
                for t in half_tiles(a):
                    dve.bn_aggr(gmv[:, t, :], gst[:, t, :]).then_inc(g_moments, 1)

            gated_stats_of(last - 1, half_tiles(0))
            half_attention_low(1)
            dve.wait_ge(res_in, (last + 1) * 16)
            half_residual(0)
            half_attention(1)
            half_attention_stats(1)
            half_mix_in(0)
            gated_stats_of(last - 1, half_tiles(1))
            gated_moments(last - 1)
            half_residual(1)
            half_differences(0)
            half_mix(0, 0)
            half_mix_in(1)
            half_mix(0, 1)
            half_differences(1)
            half_mix(1, 0)
            half_mix(1, 1)
            for t in range(NT):
                dve.wait_ge(g_normed, (last - 1) * NT + t + 1)
                dve.tensor_tensor(gate[:, t, :], gate[:, t, :], res[:, t, :], ALU.add).then_inc(out_made, 1)
            half_one_plus(0)
            half_sigmoid(0, half_tiles(0))
            half_one_plus(1)
            half_sigmoid(1, half_tiles(1)[:1])
            dve.wait_ge(stored, last * 16)
            half_gated(0)
            half_gated_stats(0)
            half_sigmoid(1, half_tiles(1)[1:])
            half_gated(1)
            half_gated_stats(1)
            for a in range(2):
                if a == 1:
                    dve.wait_ge(g_rstd_made, last + 2)
                    for t in half_tiles(a):
                        dve.tensor_scalar(gate[:, t, :], gate[:, t, :], gmv[:, t, 0:1], grstd[:, t:t + 1],
                                          ALU.subtract, ALU.mult).then_inc(g_normed, 1)
                for t in half_tiles(a):
                    dve.wait_ge(g_normed, last * NT + t + 1)
                    dve.tensor_tensor(gate[:, t, :], gate[:, t, :], last_res[:, t, :], ALU.add).then_inc(out_made, 1)

        @block.tensor
        def _(pe):
            def three(out_, a_hi, a_lo, b_hi, b_lo, start, stop):
                pe.matmul(out_, a_hi, b_hi, start=start, stop=False)
                pe.matmul(out_, a_hi, b_lo, start=False, stop=False)
                return pe.matmul(out_, a_lo, b_hi, start=False, stop=stop)

            def two(out_, a_hi, a_lo, b, start, stop):
                pe.matmul(out_, a_hi, b, start=start, stop=False)
                return pe.matmul(out_, a_lo, b, start=False, stop=stop)

            def turn_x(n, i, banks):
                pe.wait_ge(xn_made, n + 1)
                for t in range(NT):
                    for band in range(HALVES):
                        mm = pe.transpose(banks[band][:, t * P:(t + 1) * P],
                                          xin[:, i, t, band * P:(band + 1) * P], ident[:, :])
                mm.then_inc(x_turned, 1)

            def queries(j, banks):
                tokens = bass.ds(j * BLK, BLK)
                for m in range(HALVES):
                    cols = slice(m * P, (m + 1) * P)
                    two(banks[m][:, :], wt_hi[:, QK, 0, cols], wt_lo[:, QK, 0, cols], xt_low[:, tokens], True, False)
                    three(banks[m][:, :], wt_hi[:, QK, 1, cols], wt_lo[:, QK, 1, cols], xt_hi[:, tokens],
                          xt_lo[:, tokens], False, True).then_inc(q_done, 1)

            def next_batch(b):
                pe.wait_ge(xt_low_made, b * NJ + 1)
                pe.wait_ge(xt_lo_made, b * NJ + 1)
                pe.wait_ge(gated_made, (b * NJ - 1) * 2)
                queries(0, M)
                turn_x(b * NJ + 1, 1, S[2:])
                pe.wait_ge(y_lo_made, b * NJ * HALVES)
                turn_x(b * NJ + 2, 2, Y)

            def scores(g, u, first):
                t, c = unit(u, first)
                if u >= 4:
                    pe.wait_ge(s_copied, g * UNITS + u - 3)
                rows, cols = slice(t * P, (t + 1) * P), slice(c * BLK, (c + 1) * BLK)
                bank = S[u % 4][:, :]
                pe.matmul(bank, q_hi[:, 0, rows], xt_low[:, cols], start=True, stop=False)
                pe.matmul(bank, q_hi[:, 1, rows], xt_hi[:, cols], start=False, stop=False)
                pe.matmul(bank, q_hi[:, 1, rows], xt_lo[:, cols], start=False, stop=False)
                if u == 0:
                    pe.wait_ge(q_lo_made, (g + 1) * HALVES)
                pe.matmul(bank, q_lo[:, 0, rows], xt_low[:, cols], start=False, stop=False)
                pe.matmul(bank, q_lo[:, 1, rows], xt_hi[:, cols], start=False, stop=True).then_inc(s_done, 1)

            def turn_first_probs(g):
                pe.wait_ge(s_copied, (g + 1) * UNITS)
                pe.wait_ge(exp_made, g * EXPS + NT - 1)
                for kt in range(2):
                    for t in range(NT - 1):
                        pe.transpose(T[kt][:, t * P:(t + 1) * P], probs[:, t, kt * P:(kt + 1) * P], ident[:, :])
                pe.wait_ge(exp_made, g * EXPS + NT)
                t = NT - 1
                for kt in range(2):
                    pe.transpose(T[kt][:, t * P:(t + 1) * P], probs[:, t, kt * P:(kt + 1) * P],
                                 ident[:, :]).then_inc(p_turned, 1)

            def turn_probs(g, kt):
                if kt == 0:
                    pe.wait_ge(exp_made, g * EXPS + NT)
                if kt == NC:
                    pe.wait_ge(exp_made, (g + 1) * EXPS)
                for t in range(NT):
                    mm = pe.transpose(T[kt % 4][:, t * P:(t + 1) * P], probs[:, t, kt * P:(kt + 1) * P], ident[:, :])
                mm.then_inc(p_turned, 1)

            def by_rows(a_hi, a_lo, w, done):
                for t in range(NT):
                    rows = slice(t * P, (t + 1) * P)
                    for h in range(HALVES):
                        mm = three(M[t // 2][:, (t % 2) * D:(t % 2 + 1) * D], a_hi[:, h, rows], a_lo[:, h, rows],
                                   wt_hi[:, w, h, :], wt_lo[:, w, h, :], h == 0, h == HALVES - 1)
                    if t % 2:
                        mm.then_inc(done, 1)

            def project_out(p):
                pe.wait_ge(y_lo_made, p * 2 + 2)
                by_rows(yk_hi, yk_lo, OUT, o_done)

            def turn_mix_in(p):
                pe.wait_ge(mix_in_made, p * NT + NT)
                for h in range(HALVES):
                    for t in range(NT):
                        mm = pe.transpose(M[h][:, t * P:(t + 1) * P], att[:, t, h * P:(h + 1) * P], ident[:, :])
                    mm.then_inc(mix_in_turned, 1)

            def mix_keys(p):
                pe.wait_ge(xm_lo_made, p * 4 + 4)
                pe.wait_ge(rec_exp, p * 2 + 2)
                for m in range(HALVES):
                    cols = slice(m * P, (m + 1) * P)
                    for h in range(HALVES):
                        mm = three(M[m][:, :], wt_hi[:, KEY, h, cols], wt_lo[:, KEY, h, cols], xm_hi[:, 1, h, :],
                                   xm_lo[:, 1, h, :], h == 0, h == HALVES - 1)
                    mm.then_inc(key_done, 1)

            def half_rows(a, to, a_hi, a_lo, w, done):
                for t in half_tiles(a):
                    rows, cols = slice(t * P, (t + 1) * P), slice((t % PT) * D, (t % PT + 1) * D)
                    for h in range(HALVES):
                        mm = three(to[:, cols], a_hi[:, h, rows], a_lo[:, h, rows],
                                   wt_hi[:, w, h, :], wt_lo[:, w, h, :], h == 0, h == HALVES - 1)
                mm.then_inc(done, 1)

            def receptance(p):
                pe.wait_ge(xm_lo_made, p * 4 + 2)
                by_rows(xm_hi[:, 0], xm_lo[:, 0], REC, rec_done)

            def mix_values(p):
                pe.wait_ge(sq_lo_made, p * 2 + 2)
                by_rows(yk_hi, yk_lo, VAL, val_done)

            sources = [[stage_qkv[e][:, w * D:(w + 1) * D] for e in range(HALVES)] for w in range(3)]
            sources += [[stage_w[:, w, e] for e in range(HALVES)] for w in range(4)]

            def turn_weight(i):
                for h in range(HALVES):
                    for e in range(HALVES):
                        mm = pe.transpose(W_BANKS[i][:, h * D + e * P:h * D + (e + 1) * P],
                                          sources[i][e][:, h * P:(h + 1) * P], ident[:, :])
                mm.then_inc(w_turned, 1)

            def multiply_weights(a, b, to):
                pe.wait_ge(w_copied, b + 1)
                for e in range(HALVES):
                    for h in range(HALVES):
                        mm = pe.matmul(to[:, e * D:(e + 1) * D], turned_w[:, a, h, e * P:(e + 1) * P],
                                       turned_w[:, b, h, :], start=h == 0, stop=h == HALVES - 1)
                mm.then_inc(w_multiplied, 1)

            def score_stage(g, post, first, next_query, next_b=None):
                p = g - 1
                pe.wait_ge(q_hi_made, (g + 1) * HALVES)
                for u in range(UNITS):
                    if first is not None and u in (2, 4, 6):
                        pe.wait_ge(xt_low_made, first * NJ + u // 2 + 1)
                        pe.wait_ge(xt_lo_made, first * NJ + u // 2 + 1)
                    scores(g, u, first)
                    if first is not None:
                        if u == 2 and not post:
                            turn_x(first * NJ + 2, 2, Y)
                        if u == 3 and not post:
                            pe.wait_ge(s_copied, 1)
                            multiply_weights(2, 3, OUT_BANK)
                        if u == (0 if post else 3):
                            turn_x(first * NJ + 3, 3, M)
                        if u == 3 and not post:
                            pe.wait_ge(w_lo_made, 2)
                        if u == 3 and post:
                            pe.wait_ge(xt_low_made, (first + 1) * NJ)
                            pe.wait_ge(xt_lo_made, (first + 1) * NJ)
                        if u == 6 and not post:
                            pe.wait_ge(w_in, (len(STAGED) - 1) * 16)
                            for i in range(4, len(sources)):
                                turn_weight(i)
                    if post and u == (2 if first is None else 3):
                        project_out(p)
                if next_query is not None or next_b is not None:
                    pe.wait_ge(s_copied, g * UNITS + UNITS - 2)
                if next_query is not None:
                    queries(next_query, S)
                if next_b is not None:
                    turn_x(next_b * NJ, 0, S)

            def value_stage(g, post, first, next_query, next_b=None):
                p = g - 1
                if next_b is not None:
                    turn_first_probs(g)
                else:
                    for kt in range(2):
                        turn_probs(g, kt)
                if post:
                    turn_mix_in(p)
                else:
                    pe.wait_ge(w_lo_made, len(SPLIT))
                for kt in range(NKT):
                    if first is not None and kt % NT == 0:
                        pe.wait_ge(v_lo_made, first * NJ + kt // NT + 1)
                    s = kt % RING
                    low, mid = slice(0, P), slice(P, D)
                    pe.wait_ge(pt_hi_made, g * NKT + kt + 1)
                    pe.matmul(Y[0][:, :], v_hi[:, kt, low], pt_hi[:, s, :], start=kt == 0, stop=False)
                    pe.matmul(Y[1][:, :], v_lo[:, kt, :], pt_hi[:, s, :], start=kt == 0, stop=False)
                    pe.matmul(Y[1][:, :], v_hi[:, kt, mid], pt_hi[:, s, :], start=False, stop=False)
                    pe.wait_ge(pt_lo_made, g * NKT + kt + 1)
                    pe.matmul(Y[1][:, :], v_hi[:, kt, mid], pt_lo[:, s, :], start=False, stop=kt == NKT - 1)
                    pe.matmul(Y[0][:, :], v_hi[:, kt, low], pt_lo[:, s, :], start=False,
                              stop=kt == NKT - 1).then_inc(pv_done, 1)
                    if kt == 0:
                        if next_query is not None:
                            pe.wait_ge(q_lo_made, (g + 1) * HALVES + 1)
                        if next_b is not None:
                            pe.wait_ge(xt_low_made, next_b * NJ + 1)
                        turn_probs(g, 2)
                        if next_query is not None:
                            pe.wait_ge(q_lo_made, (g + 2) * HALVES)
                        if next_b is not None:
                            pe.wait_ge(xt_lo_made, next_b * NJ + 1)
                    if kt + AHEAD < NKT:
                        turn_probs(g, kt + AHEAD)
                    if post:
                        if kt == 6:
                            receptance(p)
                        if kt == 8:
                            mix_keys(p)
                        if kt == 12:
                            mix_values(p)

            def last_values():
                p = last - 1

                def turn(s):
                    a, pair_ = divmod(s, STEPS)
                    if s == 0:
                        pe.wait_ge(exp_made, last * EXPS + PT)
                    if s == STEPS:
                        pe.wait_ge(exp_made, (last + 1) * EXPS)
                    if s < 4:
                        pe.wait_ge(s_copied, last * UNITS + UNITS - 3 + s)
                    for i in range(2):
                        kt = 2 * pair_ + i
                        for t in half_tiles(a):
                            at = i * HALF + (t % PT) * P
                            mm = pe.transpose(S[s % 4][:, at:at + P], probs[:, t, kt * P:(kt + 1) * P], ident[:, :])
                    mm.then_inc(p_turned, 1)

                for s in range(AHEAD):
                    turn(s)
                for s in range(2 * STEPS):
                    a, pair_ = divmod(s, STEPS)
                    low, mid = slice(0, P), slice(P, D)
                    if s == STEPS:
                        pe.wait_ge(y_lo_made, (last + 1) * HALVES)
                    pe.wait_ge(pt_hi_made, last * NKT + s + 1)
                    for i in range(2):
                        kt, cols = 2 * pair_ + i, slice(i * HALF, (i + 1) * HALF)
                        part = pt_hi[:, s % RING, cols]
                        pe.matmul(Y[0][:, 0:HALF], v_hi[:, kt, low], part, start=kt == 0, stop=False)
                        pe.matmul(Y[1][:, 0:HALF], v_lo[:, kt, :], part, start=kt == 0, stop=False)
                        pe.matmul(Y[1][:, 0:HALF], v_hi[:, kt, mid], part, start=False, stop=False)
                    pe.wait_ge(pt_lo_made, last * NKT + s + 1)
                    for i in range(2):
                        kt, cols = 2 * pair_ + i, slice(i * HALF, (i + 1) * HALF)
                        part = pt_lo[:, s % RING, cols]
                        pe.matmul(Y[1][:, 0:HALF], v_hi[:, kt, mid], part, start=False, stop=kt == NKT - 1)
                        mm = pe.matmul(Y[0][:, 0:HALF], v_hi[:, kt, low], part, start=False, stop=kt == NKT - 1)
                    mm.then_inc(pv_done, 1)
                    if s + AHEAD < 2 * STEPS:
                        turn(s + AHEAD)
                    if s == 0:
                        turn_mix_in(p)
                    if s == STEPS - 2:
                        receptance(p)
                    if s == STEPS - 1:
                        mix_keys(p)
                    if s == A_STEP:
                        pe.wait_ge(relu_made, p * 2 + 1)
                        half_rows(0, M[0], q_hi, q_lo, OUT, o_done)
                    if s == A_STEP + 3:
                        pe.wait_ge(att_made, last * NT + PT)
                        mix_values(p)

            pe.wait_ge(ident_made, 1)
            pe.wait_ge(w_rounded, 1)
            turn_weight(0)
            turn_weight(1)
            multiply_weights(0, 1, QK_BANK)
            turn_x(0, 0, S[:2])
            pe.wait_ge(w_rounded, 2)
            turn_weight(2)
            turn_weight(3)
            pe.wait_ge(w_lo_made, 1)
            pe.wait_ge(xt_low_made, 1)
            pe.wait_ge(xt_lo_made, 1)
            queries(0, M)
            pe.wait_ge(w_copied, 4)
            turn_x(1, 1, S[2:])
            score_stage(0, False, 0, 1)
            value_stage(0, False, 0, 1)
            score_stage(1, True, None, 2)
            value_stage(1, True, None, 2)
            with pe.Fori(0, NB - 1) as b:
                for j in range(2, NJ):
                    following = j + 1 if j + 1 < NJ else None
                    next_b = b + 1 if following is None else None
                    score_stage(b * NJ + j, True, None, following, next_b)
                    value_stage(b * NJ + j, True, None, following, next_b)
                next_batch(b + 1)
                score_stage(b * NJ + NJ, True, b + 1, 1)
                value_stage(b * NJ + NJ, True, b + 1, 1)
                score_stage(b * NJ + NJ + 1, True, None, 2)
                value_stage(b * NJ + NJ + 1, True, None, 2)
            score_stage(last - 1, True, None, NJ - 1)
            value_stage(last - 1, True, None, NJ - 1)
            score_stage(last, True, None, None)
            last_values()
            pe.wait_ge(y_lo_made, (last + 2) * HALVES)
            pe.wait_ge(gated_made, last * 2)
            half_rows(1, M[1], q_hi, q_lo, OUT, o_done)
            for a in range(2):
                pe.wait_ge(mix_in_made, last * NT + (a + 1) * PT)
                for h in range(HALVES):
                    for t in half_tiles(a):
                        cols = slice((h * PT + t % PT) * P, (h * PT + t % PT + 1) * P)
                        mm = pe.transpose(Y[a][:, cols], att[:, t, h * P:(h + 1) * P], ident[:, :])
                mm.then_inc(mix_in_turned, 1)
            for a in range(2):
                c = half_cols(a)
                pe.wait_ge(xm_lo_made, last * 4 + a * 4 + 2)
                half_rows(a, S[2 + a], xm_hi[:, 0], xm_lo[:, 0], REC, rec_done)
                pe.wait_ge(xm_lo_made, last * 4 + a * 4 + 4)
                for m in range(HALVES):
                    cols = slice(m * P, (m + 1) * P)
                    for h in range(HALVES):
                        mm = three(pair(S[a][:, :])[:, m, :], wt_hi[:, KEY, h, cols], wt_lo[:, KEY, h, cols],
                                   xm_hi[:, 1, h, c], xm_lo[:, 1, h, c], h == 0, h == HALVES - 1)
                mm.then_inc(key_done, 1)
            for a in range(2):
                pe.wait_ge(sq_lo_made, last * 2 + (a + 1) * 2)
                half_rows(a, M[a], yk_hi, yk_lo, VAL, val_done)


_INS = ["L0_attn_x", "L0_attn_weight_qkv", "L0_attn_out_w", "L0_attn_out_b", "L0_ffn_W_r", "L0_ffn_W_k",
        "L0_ffn_W_v", "L0_ffn_mu_r", "L0_ffn_mu_k"]


def kernel(**inputs):
    import numpy as np
    import concourse.bacc as bacc
    from concourse.bass_utils import run_bass_kernel_spmd

    nc = bacc.Bacc("TRN2", target_bir_lowering=False, num_devices=1)
    arrays, args = {}, []
    for name in _INS:
        a = np.ascontiguousarray(inputs[name])
        arrays[f"in_{name}"] = a
        args.append(nc.dram_tensor(f"in_{name}", a.shape, mybir.dt.from_np(a.dtype), kind="ExternalInput").ap())
    shape = arrays["in_L0_attn_x"].shape
    out = nc.dram_tensor("out_x", shape, F32, kind="ExternalOutput").ap()
    sandwich(nc, *args, out)
    r = run_bass_kernel_spmd(nc, [arrays], core_ids=[0])
    return r.results[0]["out_x"]
```
